# Optimizing a Trainium2 kernel written in Bass

```python
import numpy as np
import jax
import jax.numpy as jnp

def _softmax(x, axis=-1):
    return jax.nn.softmax(x, axis=axis)

def _gelu(x):
    return jax.nn.gelu(x, approximate=True)

def _silu(x):
    return jax.nn.silu(x)

def _sigmoid(x):
    return jax.nn.sigmoid(x)

def _layernorm(x, axis=-1, eps=1e-05):
    m = jnp.mean(x, axis=axis, keepdims=True)
    v = jnp.var(x, axis=axis, keepdims=True)
    return (x - m) / jnp.sqrt(v + eps)

def _scatter_add(tgt, idx, src, axis=0):
    return tgt.at[idx].add(src)

def _segment_sum(src, seg, n):
    return jax.ops.segment_sum(src, seg, n)
kernel_name = 'mk_hybrid_d1_jaxref_r8_9f1d19'

def setup_inputs(seed: int=0):
    np.random.seed(seed)
    _w = jnp.asarray

    def _L0_attn_a_setup():
        import jax, jax.numpy as jnp
        import numpy as np
        HIDDEN = 256
        HEADS = 16
        HEAD_DIM = HIDDEN // HEADS
        key = jax.random.key(seed)
        ks = jax.random.split(key, 9)
        B, S = (1, 512)
        scale = 1.0 / np.sqrt(HIDDEN)
        x = jax.random.normal(ks[0], (B, S, HIDDEN), dtype=jnp.float32)
        Wq = jax.random.normal(ks[1], (HIDDEN, HIDDEN), dtype=jnp.float32) * scale
        Wk = jax.random.normal(ks[2], (HIDDEN, HIDDEN), dtype=jnp.float32) * scale
        Wv = jax.random.normal(ks[3], (HIDDEN, HIDDEN), dtype=jnp.float32) * scale
        Wo = jax.random.normal(ks[4], (HIDDEN, HIDDEN), dtype=jnp.float32) * scale
        bq = jax.random.normal(ks[5], (HIDDEN,), dtype=jnp.float32) * 0.01
        bk = jax.random.normal(ks[6], (HIDDEN,), dtype=jnp.float32) * 0.01
        bv = jax.random.normal(ks[7], (HIDDEN,), dtype=jnp.float32) * 0.01
        bo = jax.random.normal(ks[8], (HIDDEN,), dtype=jnp.float32) * 0.01
        return {'x': x, 'Wq': Wq, 'bq': bq, 'Wk': Wk, 'bk': bk, 'Wv': Wv, 'bv': bv, 'Wo': Wo, 'bo': bo}
    _L0_attn_a_in = _L0_attn_a_setup()

    def _L0_attn_b_setup():
        import jax, jax.numpy as jnp
        import numpy as np
        DECAY = 0.95

        def smear(x, decay):
            a = jnp.full_like(x, decay)

            def combine(c1, c2):
                a1, b1 = c1
                a2, b2 = c2
                return (a1 * a2, a2 * b1 + b2)
            _, y = jax.lax.associative_scan(combine, (a, x), axis=1)
            return y
        key = jax.random.key(seed)
        ks = jax.random.split(key, 5)
        B, S, E, M = (4, 512, 256, 256)
        x = jax.random.normal(ks[0], (B, S, E), dtype=jnp.float32)
        s = 0.02
        Wv = jax.random.normal(ks[1], (E, M), dtype=jnp.float32) * s
        Wg = jax.random.normal(ks[2], (E, M), dtype=jnp.float32) * s
        bg = jnp.zeros((M,), dtype=jnp.float32)
        Wq = jax.random.normal(ks[3], (E, M), dtype=jnp.float32) * s
        bq = jnp.zeros((M,), dtype=jnp.float32)
        Wo = jax.random.normal(ks[4], (M, E), dtype=jnp.float32) * s
        return {'x': x, 'Wv': Wv, 'Wg': Wg, 'bg': bg, 'Wq': Wq, 'bq': bq, 'Wo': Wo}
    _L0_attn_b_in = _L0_attn_b_setup()

    def _L0_ffn_setup():
        import jax, jax.numpy as jnp
        import numpy as np
        B, S, D, H = (4, 256, 256, 1024)

        def fwht(x):
            orig_shape = x.shape
            n = orig_shape[-1]
            x = x.reshape(-1, n)
            h = 1
            while h < n:
                xb = x.reshape(-1, n // (2 * h), 2, h)
                a = xb[:, :, 0, :]
                b = xb[:, :, 1, :]
                x = jnp.stack([a + b, a - b], axis=2).reshape(-1, n)
                h *= 2
            scale = jnp.asarray(1.0 / np.sqrt(n), dtype=x.dtype)
            return (x * scale).reshape(orig_shape)
        key = jax.random.key(seed)
        kx, k1, k2, k3 = jax.random.split(key, 4)
        x = jax.random.normal(kx, (B, S, D), dtype=jnp.float32)
        W1 = jax.random.normal(k1, (H, D), dtype=jnp.float32) * (1.0 / np.sqrt(D))
        W2 = jax.random.normal(k2, (D, H), dtype=jnp.float32) * (1.0 / np.sqrt(H))
        W3 = jax.random.normal(k3, (H, D), dtype=jnp.float32) * (1.0 / np.sqrt(D))
        return {'x': x, 'W1': W1, 'W2': W2, 'W3': W3}
    _L0_ffn_in = _L0_ffn_setup()
    _d = {'L0_attn_a_x': _L0_attn_a_in['x'], 'L0_attn_a_Wq': _L0_attn_a_in['Wq'], 'L0_attn_a_bq': _L0_attn_a_in['bq'], 'L0_attn_a_Wk': _L0_attn_a_in['Wk'], 'L0_attn_a_bk': _L0_attn_a_in['bk'], 'L0_attn_a_Wv': _L0_attn_a_in['Wv'], 'L0_attn_a_bv': _L0_attn_a_in['bv'], 'L0_attn_a_Wo': _L0_attn_a_in['Wo'], 'L0_attn_a_bo': _L0_attn_a_in['bo'], 'L0_attn_b_Wv': _L0_attn_b_in['Wv'], 'L0_attn_b_Wg': _L0_attn_b_in['Wg'], 'L0_attn_b_bg': _L0_attn_b_in['bg'], 'L0_attn_b_Wq': _L0_attn_b_in['Wq'], 'L0_attn_b_bq': _L0_attn_b_in['bq'], 'L0_attn_b_Wo': _L0_attn_b_in['Wo'], 'L0_ffn_W1': _L0_ffn_in['W1'], 'L0_ffn_W2': _L0_ffn_in['W2'], 'L0_ffn_W3': _L0_ffn_in['W3']}
    _x0 = _d['L0_attn_a_x']
    _d['L0_attn_a_x'] = jax.random.normal(jax.random.fold_in(jax.random.key(seed), 1), (4, 512, 256), dtype=_x0.dtype)
    del _x0
    return _d

def reference(L0_attn_a_x, L0_attn_a_Wq, L0_attn_a_bq, L0_attn_a_Wk, L0_attn_a_bk, L0_attn_a_Wv, L0_attn_a_bv, L0_attn_a_Wo, L0_attn_a_bo, L0_attn_b_Wv, L0_attn_b_Wg, L0_attn_b_bg, L0_attn_b_Wq, L0_attn_b_bq, L0_attn_b_Wo, L0_ffn_W1, L0_ffn_W2, L0_ffn_W3):

    def _L0_attn_a_ref(x, Wq, bq, Wk, bk, Wv, bv, Wo, bo):
        import jax, jax.numpy as jnp
        import numpy as np
        HIDDEN = 256
        HEADS = 16
        HEAD_DIM = HIDDEN // HEADS
        B, S, D = x.shape
        H, Hd = (HEADS, HEAD_DIM)
        Q = (x @ Wq.T + bq).reshape(B, S, H, Hd).transpose(0, 2, 1, 3)
        K = (x @ Wk.T + bk).reshape(B, S, H, Hd).transpose(0, 2, 1, 3)
        V = (x @ Wv.T + bv).reshape(B, S, H, Hd).transpose(0, 2, 1, 3)
        scores = jnp.einsum('bhqd,bhkd->bhqk', Q, K) / jnp.sqrt(jnp.float32(Hd))
        attn = jax.nn.softmax(scores, axis=-1)
        out = jnp.einsum('bhqk,bhkd->bhqd', attn, V)
        out = out.transpose(0, 2, 1, 3).reshape(B, S, D)
        return out @ Wo.T + bo

    def _L0_attn_b_ref(x, Wv, Wg, bg, Wq, bq, Wo):
        import jax, jax.numpy as jnp
        import numpy as np
        DECAY = 0.95

        def smear(x, decay):
            a = jnp.full_like(x, decay)

            def combine(c1, c2):
                a1, b1 = c1
                a2, b2 = c2
                return (a1 * a2, a2 * b1 + b2)
            _, y = jax.lax.associative_scan(combine, (a, x), axis=1)
            return y
        scale = jnp.float32(np.sqrt(1.0 - DECAY))
        gate = jax.nn.sigmoid(jnp.einsum('bse,em->bsm', x, Wg) + bg)
        store = jnp.einsum('bse,em->bsm', x, Wv) * gate * scale
        mem = smear(store, DECAY)
        que = jax.nn.sigmoid(jnp.einsum('bse,em->bsm', x, Wq) + bq)
        load = mem * que * scale
        return jnp.einsum('bsm,me->bse', load, Wo)

    def _L0_ffn_ref(x, W1, W2, W3):
        import jax, jax.numpy as jnp
        import numpy as np
        B, S, D, H = (4, 256, 256, 1024)

        def fwht(x):
            orig_shape = x.shape
            n = orig_shape[-1]
            x = x.reshape(-1, n)
            h = 1
            while h < n:
                xb = x.reshape(-1, n // (2 * h), 2, h)
                a = xb[:, :, 0, :]
                b = xb[:, :, 1, :]
                x = jnp.stack([a + b, a - b], axis=2).reshape(-1, n)
                h *= 2
            scale = jnp.asarray(1.0 / np.sqrt(n), dtype=x.dtype)
            return (x * scale).reshape(orig_shape)
        up_gate = jnp.einsum('bsd,hd->bsh', x, W1)
        up_lin = jnp.einsum('bsd,hd->bsh', x, W3)
        hidden = jax.nn.silu(up_gate) * up_lin
        hidden = fwht(hidden)
        out = jnp.einsum('bsh,dh->bsd', hidden, W2)
        return out
    x = L0_attn_a_x
    x = x + _L0_attn_a_ref(_layernorm(x, axis=-1), L0_attn_a_Wq, L0_attn_a_bq, L0_attn_a_Wk, L0_attn_a_bk, L0_attn_a_Wv, L0_attn_a_bv, L0_attn_a_Wo, L0_attn_a_bo)
    x = x + _L0_ffn_ref(_layernorm(x, axis=-1), L0_ffn_W1, L0_ffn_W2, L0_ffn_W3)
    x = x + _L0_attn_b_ref(_layernorm(x, axis=-1), L0_attn_b_Wv, L0_attn_b_Wg, L0_attn_b_bg, L0_attn_b_Wq, L0_attn_b_bq, L0_attn_b_Wo)
    x = x + _L0_ffn_ref(_layernorm(x, axis=-1), L0_ffn_W1, L0_ffn_W2, L0_ffn_W3)
    return x

_drawn_inputs = setup_inputs


def setup_inputs(seed=0):
    import zlib

    import numpy as np

    out = dict(_drawn_inputs(seed))
    spreads = {'L0_attn_b_bg': (0.0, 0.8), 'L0_attn_b_bq': (0.0, 0.8)}
    factors = {'L0_attn_a_bq': 35.527,
     'L0_attn_a_bk': 64.0,
     'L0_attn_a_bv': 4.592,
     'L0_attn_a_bo': 4.596,
     'L0_attn_b_Wv': 8.0,
     'L0_attn_b_Wg': 8.0,
     'L0_attn_b_Wq': 8.0,
     'L0_attn_b_Wo': 8.0}
    for name, (base, spread) in spreads.items():
        noise = np.random.default_rng([zlib.crc32(name.encode()), seed]).standard_normal(out[name].shape)
        drawn = base * np.exp(spread * noise) if base else spread * noise
        out[name] = jnp.asarray(drawn.astype(out[name].dtype))
    for name, factor in factors.items():
        out[name] = (out[name] * factor).astype(out[name].dtype)
    return out
```

```python
from contextlib import ExitStack

import concourse.bass as bass
from concourse import mybir

F32 = mybir.dt.float32
F32R = mybir.dt.float32r
ALU = mybir.AluOpType
ACT = mybir.ActivationFunctionType
AX = mybir.AxisListType

P = 128
BATCH, SEQ, D = 4, 512, 256
HEADS, HD = 16, 16
HID = 1024
TT = SEQ // P
KD = D // P
GROUPS = 4
GH = HEADS // GROUPS
FT = HID // P
SLOTS = GROUPS * TT * GH
AHEAD = 24
TURN = 17
QROWS = 4 * HD
MROW = 96
DMA = 16
EPS = 1e-5
DECAY = 0.95
MSCALE = float((1.0 - DECAY) ** 0.5)
QI, KI = 0, 1


def build(nc, x, wq, wk, wv, wo, bqk_d, bv, bo, mv_, mg, mq, bgq_d, mo, w1, w2, w3, ident_d, had_d, out):
    ctx = ExitStack()
    with ctx:
        def sb(name, shape, dt=F32):
            return ctx.enter_context(nc.sbuf_tensor(name, shape, dt))

        def sem(name):
            return ctx.enter_context(nc.semaphore(name))

        X = sb("X", [P, BATCH * TT, D])
        XNs = sb("XNs", [P, TT, D])
        xf = sb("xf", [P, KD, SEQ])
        xTh = sb("xTh", [P, 2, KD, SEQ], F32R)
        xTl = sb("xTl", [P, 2, KD, SEQ], F32R)
        ring = sb("ring", [P, GROUPS, 2, GH, SEQ], F32R)
        PR = sb("PR", [P, 8, SEQ])
        Vp = sb("Vp", [P, TT, HEADS, 2 * HD])
        vst = sb("vst", [P, TT, D])
        qf = sb("qf", [P, 2, SEQ])
        qh = sb("qh", [P, 2, SEQ], F32R)
        ql = sb("ql", [P, 2, SEQ], F32R)
        OT = sb("OT", [P, SEQ // 32, 32])
        OTn = sb("OTn", [P, SEQ // 32, 32])
        AOf = sb("AOf", [P, SEQ])
        AOh = sb("AOh", [P, GROUPS, SEQ], F32R)
        AOl = sb("AOl", [P, GROUPS, SEQ], F32R)
        WAh = sb("WAh", [P, 3, KD, D], F32R)
        WAl = sb("WAl", [P, 3, KD, D], F32R)
        WOh = sb("WOh", [P, GROUPS, D], F32R)
        WOl = sb("WOl", [P, GROUPS, D], F32R)
        bqk = sb("bqk", [P, 4])
        bgq = sb("bgq", [P, 4])
        bvt = sb("bvt", [P, D])
        bot = sb("bot", [P, D])
        ident = sb("ident", [P, P])
        had = sb("had", [P, P])
        mxr = sb("mxr", [P, GH * TT])
        ms = sb("ms", [P, 2, GH * TT])
        mT = sb("mT", [P, 32])
        rec = sb("rec", [P, SEQ // 32])
        bst = sb("bst", [P, BATCH * TT, 6])
        mom = sb("mom", [P, BATCH * TT, 2])
        veps = sb("veps", [P, BATCH * TT])
        rstd = sb("rstd", [P, BATCH * TT])
        eps = sb("eps", [P, BATCH * TT])
        mhalf = sb("mhalf", [P, BATCH * TT])
        decay = sb("decay", [P, 1])
        spare = sb("spare", [P, 1])
        credit = sb("credit", [P, 1])
        PS = ctx.enter_context(nc.psum_tensor("PS", [P, 8, SEQ], F32))
        OB, MB = PS[:, 6, :], PS[:, 7, :]
        qscr = nc.dram_tensor("qk_scratch", [BATCH, 2, 2, 2, HD, HEADS // 2, SEQ], F32, kind="Internal").ap()
        mscr = nc.dram_tensor("max_scratch", [GROUPS, 2 * GH * TT, P // 32, 32], F32, kind="Internal").ap()
        wscr = nc.dram_tensor("weight_scratch", [4, P, 2, KD * HID], F32, kind="Internal").ap()
        W_UP, W_LIN, W_DOWN, W_MEM = range(4)

        def parts(slot):
            v = ring[:, slot, :, :, :].rearrange("p a h n -> p a (h n)")
            return v[:, 0, :], v[:, 1, :]

        x_in = [sem(f"x_in{b}") for b in range(BATCH)]
        wqk_in, wv_in, wo_in, bias_in, const_in = (sem(n) for n in ("wqk_in", "wv_in", "wo_in", "bias_in", "const_in"))
        raw_in = [sem("raw_in0"), sem("raw_in1")]
        zero_done, one_done, pool_init, fill_in, whi_done, wlo_done, had_ready, had_copied, fly_done, lhi_done, llo_done, wout = (
            sem(n) for n in ("zero_done", "one_done", "pool_init", "fill_in", "whi_done", "wlo_done", "had_ready", "had_copied", "fly_done",
                             "lhi_done", "llo_done", "wout"))
        bst_done, mom_done, veps_done, rstd_done, xns_ready, lnT_ready, x_hi, x_lo = (
            sem(n) for n in ("bst_done", "mom_done", "veps_done", "rstd_done", "xns_ready", "lnT_ready", "x_hi", "x_lo"))
        qk_ready, qk_hi, qk_lo, v_ready, v_copied, vp_ready, bo_added = (
            sem(n) for n in ("qk_ready", "qk_hi", "qk_lo", "v_ready", "v_copied", "vp_ready", "bo_added"))
        scr_out = [sem("scr_out0"), sem("scr_out1")]
        ring_in = [sem(f"ring_in{g}") for g in range(GROUPS)]
        s1_ready, max_done, mh_done, ml_done, mt_ready, mscr_out = (
            sem(n) for n in ("s1_ready", "max_done", "mh_done", "ml_done", "mt_ready", "mscr_out"))
        mrow_in = [sem(f"mrow_in{g}") for g in range(GROUPS)]
        st_ready, exp_done, av_done, ot_done, rec_done, otn_done, aof_ready, aoh_done, aol_done, wo_ready, x_done = (
            sem(n) for n in ("st_ready", "exp_done", "av_done", "ot_done", "rec_done", "otn_done", "aof_ready",
                             "aoh_done", "aol_done", "wo_ready", "x_done"))
        w_in = [sem(f"w_in{g}") for g in range(4)]
        g_ready, u_ready, sg_done, hf_done, hh_done, hl_done, y_ready = (
            sem(n) for n in ("g_ready", "u_ready", "sg_done", "hf_done", "hh_done", "hl_done", "y_ready"))
        bg_ready, bq_ready, bv_ready, bsg_done, bsq_done, bst2_done, scan_done, load_done, lh_done, ll_done = (
            sem(n) for n in ("bg_ready", "bq_ready", "bv_ready", "bsg_done", "bsq_done", "bst2_done", "scan_done",
                             "load_done", "lh_done", "ll_done"))
        out_done = sem("out_done")

        def windows(eng, slot, tail):
            for k in range(TURN):
                slot(0, k, True, False)
            with eng.Fori(0, BATCH - 1) as b:
                for k in range(TURN, SLOTS):
                    slot(b, k, False, False)
                for k in range(TURN):
                    slot(b + 1, k, False, False)
            for k in range(TURN, SLOTS):
                slot(BATCH - 1, k, False, True)
            tail(BATCH)

        block = ctx.enter_context(nc.Block())

        @block.sync
        def _(sp):
            xv = x.rearrange("b (t p) d -> b p t d", p=P)
            sp.dma_start(X[:, 0:TT, :], xv[0, :, :, :]).then_inc(x_in[0], DMA)
            for i, w in enumerate((wq, wk)):
                sp.dma_start(qf[:, i, :].rearrange("p (k n) -> p k n", k=KD),
                             w.rearrange("(k p) n -> p k n", p=P)).then_inc(wqk_in, DMA)
            sp.dma_start(xf[:, 0, :].rearrange("p (k n) -> p k n", k=KD),
                         wv.rearrange("(k p) n -> p k n", p=P)).then_inc(wv_in, DMA)
            sp.dma_start(ident[:, :], ident_d).then_inc(const_in, DMA)
            sp.dma_start(had[:, :], had_d).then_inc(const_in, DMA)
            sp.dma_start(PR[:, 0:4, :].rearrange("p a (u n) -> p (a u) n", n=D),
                         w2.rearrange("(f p) n -> p f n", p=P)).then_inc(raw_in[0], DMA)
            sp.dma_start(vst[:, :, :], wo.rearrange("g p n -> p g n")).then_inc(wo_in, DMA)
            sp.dma_start(bqk[:, :], bqk_d).then_inc(bias_in, DMA)
            sp.dma_start(bgq[:, :], bgq_d).then_inc(bias_in, DMA)
            sp.dma_start(bvt[:, :], bv.partition_broadcast(P)).then_inc(bias_in, DMA)
            sp.dma_start(bot[:, :], bo.partition_broadcast(P)).then_inc(bias_in, DMA)
            for b in range(1, BATCH):
                sp.dma_start(X[:, b * TT:(b + 1) * TT, :], xv[b, :, :, :]).then_inc(x_in[b], DMA)
            sp.wait_ge(zero_done, 1)
            sp.dma_start(ring[QROWS:MROW, :, :, :, :].rearrange("p g a h n -> p (g a h) n").bitcast(F32),
                         OTn[0:MROW - QROWS, :, :].rearrange("p a c -> p (a c)").unsqueeze(1)
                         .broadcast_to([MROW - QROWS, GROUPS * 2 * GH, SEQ])).then_inc(fill_in, DMA)
            sp.wait_ge(one_done, 1)
            for g in range(GROUPS):
                sp.dma_start(ring[MROW:MROW + 2, g, KI, :, :].bitcast(F32),
                             AOf[0:2, :].unsqueeze(1).broadcast_to([2, GH, SEQ])).then_inc(fill_in, DMA)

            def scratch_out(b, n):
                sp.wait_ge(qk_lo, 4 * b + n + 1)
                mt, qk = n // 2, n % 2
                for part, t in ((0, qh), (1, ql)):
                    sp.dma_start(qscr[b, qk, part, mt, :, :, :].rearrange("r h n -> (r h) n"),
                                 t[:, n % 2, :].bitcast(F32)).then_inc(scr_out[n % 2], DMA)

            def ring_load(b, g):
                mt, h0 = g // 2, GH * (g % 2)
                for qk in (QI, KI):
                    sp.wait_ge(scr_out[qk], 2 * DMA * (2 * b + mt + 1))
                    for a in range(2):
                        dst = ring[32 * a:32 * a + 32, g, qk, :, :].rearrange("p h n -> p (h n)").bitcast(F32)
                        if qk == QI:
                            src = qscr[b, qk, a, mt, :, h0:h0 + GH, :].rearrange("r h n -> r (h n)")
                            src = src.unsqueeze(0).broadcast_to([2, HD, GH * SEQ])
                        else:
                            src = qscr[b, qk, :, mt, :, h0:h0 + GH, :].rearrange("a r h n -> a r (h n)")
                        sp.dma_start(dst, src).then_inc(ring_in[g], DMA)

            def max_rows(b, g):
                sp.wait_ge(mt_ready, 4 * b + g + 1)
                sp.dma_start(mscr[g, :, :, :].rearrange("k c n -> c k n"), mT[:, :]).then_inc(mscr_out, DMA)
                sp.wait_ge(mscr_out, DMA * (4 * b + g + 1))
                sp.dma_start(ring[MROW:MROW + 2, g, QI, :, :].rearrange("p h n -> p (h n)").bitcast(F32),
                             mscr[g, :, :, :].rearrange("(a k) c n -> a (k c n)", a=2)).then_inc(mrow_in[g], DMA)

            def weights_in(w):
                sp.wait_ge(st_ready, SLOTS * (BATCH - 1) + 16 * (w + 1))
                sp.dma_start(ring[:, w, :, :, :].rearrange("p a h n -> p (a h n)").bitcast(F32),
                             wscr[w, :, :, :].rearrange("p a n -> p (a n)")).then_inc(w_in[w], DMA)

            def split_out(n, w):
                sp.wait_ge(llo_done, n + 1)
                for part, t in ((0, AOh), (1, AOl)):
                    sp.dma_start(wscr[w, :, part, :], t[:, :, :].rearrange("p g n -> p (g n)").bitcast(F32))\
                      .then_inc(wout, DMA)

            def raw_load(half, j, k, src):
                sp.dma_start(PR[:, 4 * half + j:4 * half + j + k, :].rearrange("p a n -> p (a n)")
                             .rearrange("p (k n) -> p k n", k=KD),
                             src.rearrange("(k p) n -> p k n", p=P)).then_inc(raw_in[half], DMA)

            for n in range(2):
                scratch_out(0, n)
            ring_load(0, 0)
            ring_load(0, 1)
            for n in range(2, 4):
                scratch_out(0, n)
            ring_load(0, 2)
            ring_load(0, 3)
            sp.wait_ge(fly_done, 3)
            raw_load(0, 0, 4, w1)
            split_out(0, W_DOWN)
            raw_load(1, 0, 4, w3)
            split_out(1, W_UP)
            for j, w in enumerate((mv_, mg, mq, mo)):
                raw_load(0, j, 1, w)
            split_out(2, W_LIN)
            split_out(3, W_MEM)
            max_rows(0, 0)

            def slot(b, k, first, last):
                g, i = k // 16, k % 16
                if k == 1 and not first:
                    sp.wait_ge(st_ready, SLOTS * b)
                    ring_load(b, 3)
                if i == 9 and not (last and g == 3):
                    max_rows(b + (g + 1) // GROUPS, (g + 1) % GROUPS)
                if not last:
                    if k in (27, 30, 33, 36):
                        scratch_out(b + 1, (k - 27) // 3)
                    if k in (33, 37, 49):
                        g1 = (33, 37, 49).index(k)
                        sp.wait_ge(st_ready, SLOTS * b + 16 * (g1 + 1))
                        ring_load(b + 1, g1)
                elif k in (17, 33, 49):
                    weights_in(g - 1)

            windows(sp, slot, lambda b: weights_in(W_MEM))
            ov = out.rearrange("b (t p) d -> b p t d", p=P)
            for c in range(BATCH):
                sp.wait_ge(x_done, 2 * (BATCH + 2 * BATCH + c + 1))
                sp.dma_start(ov[c, :, :, :], X[:, c * TT:(c + 1) * TT, :]).then_inc(out_done, DMA)
            sp.wait_ge(out_done, DMA * BATCH)

        @block.tensor
        def _(pe):
            def mm(dst, lhsT, rhs, start, stop):
                return nc.tensor.matmul(dst, lhsT, rhs, start=start, stop=stop, skip_group_check=True)

            def split_mm(dst, pairs, start=True, stop=True):
                n = 3 * len(pairs)
                ops = [(l, r) for ll, lh, rl, rh in pairs for l, r in ((ll, rh), (lh, rl), (lh, rh))]
                for i, (l, r) in enumerate(ops):
                    last = mm(dst, l, r, start and i == 0, stop and i == n - 1)
                return last

            def ln_transpose(L, dt, bank):
                for t in range(TT):
                    last = nc.tensor.transpose(bank[:, t * P:(t + 1) * P], XNs[:, t, dt * P:(dt + 1) * P], ident[:, :])
                last.then_inc(lnT_ready, 1)

            def xt(par, kt):
                return xTl[:, par, kt, :], xTh[:, par, kt, :]

            def project_qk(b, n, part, fresh=False):
                w, m = n % 2, n // 2 * P
                ops = [(lo, r, kt) for kt in range(KD) for lo, r in ((1, 1), (0, 0), (0, 1))]
                for i in (2 * part, 2 * part + 1):
                    lo, r, kt = ops[i]
                    lhsT = (WAl if lo else WAh)[:, w, kt, m:m + P]
                    last = mm(MB, lhsT, xt(0, kt)[r], i == 0, i == 5)
                if part == 2:
                    last.then_inc(qk_ready, 1)

            def project_v(b, half, part):
                ops = [(t, kt, l, w) for t in range(2) for kt in range(KD) for l, w in ((0, WAh), (1, WAl), (1, WAh))]
                for i in range(4 * part, 4 * part + 4):
                    t, kt, l, w = ops[i]
                    tok = (2 * half + t) * P
                    last = mm(MB[:, t * D:(t + 1) * D], xt(0, kt)[l][:, tok:tok + P], w[:, 2, kt, :],
                              i % 6 == 0, i % 6 == 5)
                if part == 2:
                    last.then_inc(v_ready, 1)

            def out_projection(b, half, part):
                ops = [(t, g, a, w) for t in range(2) for g in range(GROUPS)
                       for a, w in ((AOl, WOh), (AOh, WOl), (AOh, WOh))]
                for i in range(6 * part, 6 * part + 6):
                    t, g, a, w = ops[i]
                    tok = (2 * half + t) * P
                    last = mm(MB[:, t * D:(t + 1) * D], a[:, g, tok:tok + P], w[:, g, :], i % 12 == 0, i % 12 == 11)
                if part == 3:
                    last.then_inc(wo_ready, 1)

            def score_qk(b, kk, fresh=False):
                g, i = kk // 16, kk % 16
                j, t, pair = i // TT, i % TT, kk // 2 % 2
                if i == 0:
                    pe.wait_ge(ring_in[g], 4 * DMA * (b + 1))
                if kk % 2 == 0 and not (fresh and kk < 4):
                    pe.wait_ge(max_done, 32 * b + kk // 2 - 1)
                last = mm(PS[:, 2 + 2 * pair + t % 2, :], ring[0:MROW, g, QI, j, t * P:(t + 1) * P],
                          ring[0:MROW, g, KI, j, :], True, True)
                if kk % 2:
                    last.then_inc(s1_ready, 1)

            def score_kq(b, k, first):
                g, i = k // 16, k % 16
                kt, j = i // GH, i % GH
                if i == 0:
                    pe.wait_ge(mrow_in[g], DMA * (b + 1))
                if not (first and k < 2):
                    pe.wait_ge(exp_done, SLOTS * b + k - 1)
                mm(PS[:, k % 2, :], ring[0:MROW + 2, g, KI, j, kt * P:(kt + 1) * P], ring[0:MROW + 2, g, QI, j, :],
                   True, True).then_inc(st_ready, 1)

            def weigh_values(b, g, kt, first=False):
                s = 4 * b + g
                pe.wait_ge(exp_done, 16 * s + 4 * kt + 4)
                if kt == 0:
                    pe.wait_ge(vp_ready, s + 1)
                    if not first:
                        pe.wait_ge(ot_done, s)
                for j in range(GH):
                    last = mm(OB[32 * j:32 * j + 32, :], Vp[:, kt, GH * g + j, :], PR[:, (4 * kt + j) % 8, :],
                              kt == 0, kt == TT - 1)
                last.then_inc(av_done, 1)

            pe.wait_ge(const_in, 2 * DMA)
            pe.wait_ge(raw_in[0], DMA)
            for n in range(FT // 2):
                last = mm(PS[:, 2 + n, :], had[:, :], PR[:, n, :], True, True)
            last.then_inc(had_ready, 1)
            pe.wait_ge(xns_ready, 1)
            ln_transpose(0, 0, MB)
            pe.wait_ge(x_hi, 1)
            ln_transpose(0, 1, MB)
            pe.wait_ge(wlo_done, 3)
            pe.wait_ge(x_lo, 2)
            for n in range(4):
                if n:
                    pe.wait_ge(qk_hi, n)
                for part in range(3):
                    project_qk(0, n, part)
            pe.wait_ge(qk_hi, 4)
            for part in range(3):
                project_v(0, 0, part)
            pe.wait_ge(v_copied, 1)
            for part in range(3):
                project_v(0, 1, part)
            pe.wait_ge(fill_in, 5 * DMA)
            pe.wait_ge(had_copied, 1)
            for kk in range(AHEAD):
                score_qk(0, kk, True)

            def slot(b, k, first, last):
                g, i = k // 16, k % 16
                score_kq(b, k, first)
                kk = k + AHEAD
                if kk < SLOTS:
                    score_qk(b, kk)
                elif not last:
                    score_qk(b + 1, kk - SLOTS)
                if i % 4 == 2:
                    if i > 2:
                        weigh_values(b, g, i // 4 - 1, first and g == 0)
                    elif g:
                        weigh_values(b, g - 1, TT - 1)
                    elif not first:
                        weigh_values(b - 1, GROUPS - 1, TT - 1)
                if not first and 8 <= k < 16:
                    if k == 8:
                        pe.wait_ge(aol_done, 4 * b + 1)
                        pe.wait_ge(v_copied, 2 * b + 2)
                    if k == 12:
                        pe.wait_ge(x_done, 2 * b - 1)
                    out_projection(b - 1, (k - 8) // 4, (k - 8) % 4)
                if k == (24 if last else 18):
                    pe.wait_ge(xns_ready, b + 2)
                    ln_transpose(b + 1, 0, MB)
                if k == (26 if last else 20):
                    pe.wait_ge(x_hi, 2 * b + 3)
                    ln_transpose(b + 1, 1, MB)
                if not last:
                    if 22 <= k < 34:
                        n, part = (k - 22) // 3, (k - 22) % 3
                        if k == 22:
                            pe.wait_ge(x_hi, 2 * b + 4)
                            pe.wait_ge(x_lo, 2 * b + 4)
                        elif part == 0:
                            pe.wait_ge(qk_hi, 4 * b + 4 + n)
                        project_qk(b + 1, n, part)
                    if 35 <= k < 41:
                        half, part = (k - 35) // 3, (k - 35) % 3
                        if k == 35:
                            pe.wait_ge(qk_hi, 4 * b + 8)
                        if k == 38:
                            pe.wait_ge(v_copied, 2 * b + 3)
                        project_v(b + 1, half, part)

            def tail(b):
                weigh_values(b - 1, GROUPS - 1, TT - 1)
                pe.wait_ge(aol_done, 4 * b + 1)
                pe.wait_ge(x_hi, 2 * b + 2)
                for half in range(2):
                    if half:
                        pe.wait_ge(x_done, 2 * b - 1)
                    for part in range(4):
                        out_projection(b - 1, half, part)

            windows(pe, slot, tail)

            def ffn_chunk(p, n, f0, par, last):
                w1h, w1l = (v.rearrange("p (k n) -> p k n", k=KD) for v in parts(W_UP))
                w3h, w3l = (v.rearrange("p (k n) -> p k n", k=KD) for v in parts(W_LIN))
                w2h, w2l = (v.rearrange("p (f n) -> p f n", f=FT) for v in parts(W_DOWN))

                def down(f):
                    pe.wait_ge(hl_done, FT * f0 + f + 1)
                    for t in range(TT):
                        ts = slice(t * P, (t + 1) * P)
                        last_ = split_mm(PS[:, 4 + t // 2, t % 2 * D:(t % 2 + 1) * D],
                                         [(AOl[:, f % 2, ts], AOh[:, f % 2, ts], w2l[:, f, :], w2h[:, f, :])],
                                         f == 0 and t % 2 == 0, f == FT - 1)
                        if f == FT - 1 and t % 2:
                            last_.then_inc(y_ready, 1)

                pe.wait_ge(x_lo, 2 * (n + BATCH + 1))
                for f in range(FT):
                    fs = slice(f * P, (f + 1) * P)
                    pe.wait_ge(hf_done, FT * f0 + f + 1)
                    for bank, wl, wh, ready in ((f % 2, w1l, w1h, g_ready), (2 + f % 2, w3l, w3h, u_ready)):
                        split_mm(PS[:, bank, :], [(wl[:, k, fs], wh[:, k, fs]) + xt(par, k) for k in range(KD)])\
                            .then_inc(ready, 1)
                    if f:
                        down(f - 1)
                    if f == 4 and not last:
                        pe.wait_ge(xns_ready, n + BATCH + 2)
                        ln_transpose(n + 1, 0, PS[:, 6, :])
                        ln_transpose(n + 1, 1, PS[:, 7, :])
                down(FT - 1)

            def mem_chunk(n, par):
                wh, wl = (v.rearrange("p (w k n) -> p w k n", w=4, k=KD) for v in parts(W_MEM))
                c0 = n - BATCH
                pe.wait_ge(x_lo, 2 * (n + BATCH + 1))
                for m in range(KD):
                    if m:
                        pe.wait_ge(x_done, 2 * (n + BATCH))
                    ms_ = slice(m * P, (m + 1) * P)
                    for w, ready in ((1, bg_ready), (2, bq_ready), (0, bv_ready)):
                        split_mm(PS[:, 3 * m + w, :],
                                 [(wl[:, w, k, ms_], wh[:, w, k, ms_]) + xt(par, k) for k in range(KD)])\
                            .then_inc(ready, 1)
                pe.wait_ge(xns_ready, n + BATCH + 2)
                for dt in range(KD):
                    ln_transpose(n + 1, dt, PS[:, 6 + dt, :])
                pe.wait_ge(x_hi, 2 * (n + BATCH + 2))
                for m in range(KD):
                    pe.wait_ge(ll_done, KD * c0 + m + 1)
                    for t in range(TT):
                        ts = slice(t * P, (t + 1) * P)
                        last = split_mm(PS[:, 6 + t // 2, t % 2 * D:(t % 2 + 1) * D],
                                        [(AOl[:, m, ts], AOh[:, m, ts], wl[:, 3, m, :], wh[:, 3, m, :])],
                                        m == 0 and t % 2 == 0, m == KD - 1)
                        if m == KD - 1 and t % 2:
                            last.then_inc(y_ready, 1)

            for w in (W_UP, W_LIN, W_DOWN):
                pe.wait_ge(w_in[w], DMA)
            with pe.Fori(0, 2) as i:
                for cc in range(2):
                    if cc == 0:
                        pe.wait_ge(x_done, 2 * BATCH)
                    ffn_chunk(0, 2 * i + cc, 2 * i + cc, cc, False)
            pe.wait_ge(w_in[W_MEM], DMA)
            with pe.Fori(0, 2) as i:
                for cc in range(2):
                    mem_chunk(BATCH + 2 * i + cc, cc)
            for c in range(BATCH):
                ffn_chunk(2, 2 * BATCH + c, BATCH + c, c % 2, c == BATCH - 1)

        @block.scalar
        def _(act):
            def hi(dst, src, scale=1.0):
                return nc.scalar.activation(dst, src, ACT.Copy, scale=scale)

            def ln_evacuate(L, dt, par, bank, fresh=False):
                act.wait_ge(lnT_ready, 2 * L + dt + 1)
                if not fresh:
                    act.wait_ge(x_lo, 2 * L - 1 + dt)
                hi(xf[:, dt, :], bank)
                hi(xTh[:, par, dt, :], bank).then_inc(x_hi, 1)

            def qk_evacuate(b, n, fresh=False):
                act.wait_ge(qk_ready, 4 * b + n + 1)
                if not (fresh and n < 2):
                    act.wait_ge(scr_out[n % 2], 2 * DMA * (2 * b + n // 2))
                nc.scalar.activation(qf[:, n % 2, :], MB, ACT.Identity, bias=bqk[:, n:n + 1])
                nc.scalar.activation(qh[:, n % 2, :], MB, ACT.Identity, bias=bqk[:, n:n + 1]).then_inc(qk_hi, 1)

            def v_evacuate(b, half, fresh=False):
                act.wait_ge(v_ready, 2 * b + half + 1)
                if not fresh:
                    act.wait_ge(vp_ready, 4 * b)
                hi(vst[:, 2 * half:2 * half + 2, :].rearrange("p t n -> p (t n)"), MB).then_inc(v_copied, 1)

            act.wait_ge(wqk_in, 2 * DMA)
            for i in range(2):
                hi(WAh[:, i, :, :].rearrange("p k n -> p (k n)"), qf[:, i, :]).then_inc(whi_done, 1)
            act.wait_ge(wv_in, DMA)
            hi(WAh[:, 2, :, :].rearrange("p k n -> p (k n)"), xf[:, 0, :]).then_inc(whi_done, 1)
            act.wait_ge(wo_in, DMA)
            hi(WOh[:, :, :].rearrange("p g n -> p (g n)"), vst[:, :, :].rearrange("p t n -> p (t n)")).then_inc(whi_done, 1)
            act.wait_ge(had_ready, 1)
            for n in range(FT // 2):
                last = hi(PR[:, n, :], PS[:, 2 + n, :])
            last.then_inc(had_copied, 1)
            act.wait_ge(wlo_done, 3)
            for dt in range(KD):
                ln_evacuate(0, dt, 0, MB, True)
            act.wait_ge(bias_in, 4 * DMA)
            for n in range(4):
                qk_evacuate(0, n, True)
            act.wait_ge(wlo_done, 4)
            for half in range(2):
                v_evacuate(0, half, True)

            def split_hi(n, half, ready, count, scale=1.0):
                act.wait_ge(ready, count)
                if n:
                    act.wait_ge(wout, 2 * DMA * n)
                hi(AOh[:, :, :].rearrange("p g n -> p (g n)"),
                   PR[:, 4 * half:4 * half + 4, :].rearrange("p a n -> p (a n)"), scale).then_inc(lhi_done, 1)

            split_hi(0, 1, fly_done, 3, 1.0 / HID ** 0.5)
            split_hi(1, 0, raw_in[0], 2 * DMA)
            split_hi(2, 1, raw_in[1], DMA)
            split_hi(3, 0, raw_in[0], 6 * DMA)
            act.wait_ge(llo_done, 4)

            def slot(b, k, first, last):
                g, i = k // 16, k % 16
                act.wait_ge(st_ready, SLOTS * b + k + 1)
                if k % 4 == 0 and not (first and k < 8):
                    act.wait_ge(av_done, 16 * b + k // 4 - 1)
                nc.scalar.activation(PR[:, k % 8, :], PS[:, k % 2, :], ACT.Exp, scale=HD ** -0.5).then_inc(exp_done, 1)
                if k == TURN - 1 and first:
                    act.wait_ge(wout, 8 * DMA)
                if i == 6 and not (first and g == 0):
                    act.wait_ge(aof_ready, 4 * b + g)
                    hi(AOh[:, (g - 1) % GROUPS, :], AOf[:, :]).then_inc(aoh_done, 1)
                if k in ((25, 27) if last else (19, 21)):
                    ln_evacuate(b + 1, 0 if k in (19, 25) else 1, 0, MB)
                if not last:
                    if k in (25, 28, 31, 34):
                        qk_evacuate(b + 1, (k - 25) // 3)
                    if k in (38, 41):
                        v_evacuate(b + 1, (k - 38) // 3)

            def tail(b):
                act.wait_ge(aof_ready, 4 * b)
                hi(AOh[:, GROUPS - 1, :], AOf[:, :]).then_inc(aoh_done, 1)

            windows(act, slot, tail)

            def ffn_chunk(n, f0, par, last):
                for f in range(FT):
                    act.wait_ge(g_ready, FT * f0 + f + 1)
                    nc.scalar.activation(PR[:, f % 2, :], PS[:, f % 2, :], ACT.Silu).then_inc(sg_done, 1)
                    act.wait_ge(hf_done, FT * f0 + f + 3)
                    hi(AOh[:, f % 2, :], PR[:, 2 + f % 2, :]).then_inc(hh_done, 1)
                    if f == 5 and not last:
                        for dt in range(KD):
                            ln_evacuate(n + BATCH + 1, dt, 1 - par, PS[:, 6 + dt, :])

            def mem_chunk(n, par):
                c0 = n - BATCH
                for m in range(KD):
                    act.wait_ge(bg_ready, KD * c0 + m + 1)
                    nc.scalar.activation(PR[:, m, :], PS[:, 3 * m + 1, :], ACT.Sigmoid, bias=bgq[:, m:m + 1]).then_inc(bsg_done, 1)
                    act.wait_ge(bq_ready, KD * c0 + m + 1)
                    nc.scalar.activation(PR[:, 2 + m, :], PS[:, 3 * m + 2, :], ACT.Sigmoid, bias=bgq[:, 2 + m:3 + m]).then_inc(bsq_done, 1)
                    if m:
                        for dt in range(KD):
                            ln_evacuate(n + BATCH + 1, dt, 1 - par, PS[:, 6 + dt, :])
                    act.wait_ge(load_done, KD * c0 + m + 1)
                    hi(AOh[:, m, :], PR[:, 4 + m, :]).then_inc(lh_done, 1)

            with act.Fori(0, 2) as i:
                for cc in range(2):
                    ffn_chunk(2 * i + cc, 2 * i + cc, cc, False)
            with act.Fori(0, 2) as i:
                for cc in range(2):
                    mem_chunk(BATCH + 2 * i + cc, cc)
            for c in range(BATCH):
                ffn_chunk(2 * BATCH + c, BATCH + c, c % 2, c == BATCH - 1)

        @block.vector
        def _(dve):
            def pause():
                nc.vector.memset(spare[:, :], 0.0)

            def statistics(X0, n0, count, n):
                for t in range(count):
                    last = nc.vector.bn_stats(bst[:, n0 + t, :], X[:, X0 + t, :])
                last.then_inc(bst_done, 1)
                dve.wait_ge(bst_done, n)
                pause()
                for t in range(count):
                    last = nc.vector.bn_aggr(mom[:, n0 + t, :], bst[:, n0 + t, :])
                last.then_inc(mom_done, 1)

            def normalise(X0, n0, L, fresh=False):
                if not fresh:
                    dve.wait_ge(lnT_ready, 2 * L)
                for t in range(TT):
                    last = nc.vector.tensor_scalar(XNs[:, t, :], X[:, X0 + t, :], mom[:, bass.ds(n0 + t, 1), 0],
                                                   rstd[:, bass.ds(n0 + t, 1)], ALU.subtract, ALU.mult)
                last.then_inc(xns_ready, 1)

            def lo(dst, src, h):
                return nc.vector.tensor_tensor(dst, src, h.bitcast(F32), ALU.subtract)

            nc.vector.memset(OTn[:, :, :], 0.0).then_inc(zero_done, 1)
            nc.vector.memset(AOf[:, :], 1.0).then_inc(one_done, 1)
            nc.vector.memset(decay[:, :], DECAY)
            dve.wait_ge(x_in[0], DMA)
            statistics(0, 0, TT, 1)
            for i in range(3):
                dve.wait_ge(whi_done, i + 1)
                raw = xf[:, 0, :] if i == 2 else qf[:, i, :]
                lo(WAl[:, i, :, :].rearrange("p k n -> p (k n)"), raw, WAh[:, i, :, :].rearrange("p k n -> p (k n)"))\
                    .then_inc(wlo_done, 1)
            dve.wait_ge(rstd_done, 1)
            normalise(0, 0, 0, True)
            dve.wait_ge(whi_done, 4)
            lo(WOl[:, :, :].rearrange("p g n -> p (g n)"), vst[:, :, :].rearrange("p t n -> p (t n)"),
               WOh[:, :, :].rearrange("p g n -> p (g n)")).then_inc(wlo_done, 1)
            for b in range(1, BATCH):
                dve.wait_ge(x_in[b], DMA)
            statistics(TT, TT, (BATCH - 1) * TT, 2)
            dve.wait_ge(had_copied, 1)
            for st in range(3):
                r = 1 << st
                src, dst = (PR[:, 4 * h:4 * h + 4, :].rearrange("p a n -> p (a n)")
                            .rearrange("p (m u r) -> p m u r", u=2, r=r * D) for h in (st % 2, 1 - st % 2))
                if st:
                    dve.wait_ge(fly_done, st)
                nc.vector.tensor_tensor(dst[:, :, 0, :], src[:, :, 0, :], src[:, :, 1, :], ALU.add)
                nc.vector.tensor_tensor(dst[:, :, 1, :], src[:, :, 0, :], src[:, :, 1, :], ALU.subtract).then_inc(fly_done, 1)
            for n, half in enumerate((1, 0, 1, 0)):
                dve.wait_ge(lhi_done, n + 1)
                raw = PR[:, 4 * half:4 * half + 4, :].rearrange("p a n -> p (a n)")
                h = AOh[:, :, :].rearrange("p g n -> p (g n)")
                dst = AOl[:, :, :].rearrange("p g n -> p (g n)")
                if n:
                    lo(dst, raw, h).then_inc(llo_done, 1)
                else:
                    nc.vector.scalar_tensor_tensor(dst, raw, 1.0 / HID ** 0.5, h.bitcast(F32), ALU.mult, ALU.subtract)\
                        .then_inc(llo_done, 1)

            def row_max(b, kk):
                g, i = kk // 16, kk % 16
                dve.wait_ge(s1_ready, 32 * b + kk // 2 + 1)
                pair = kk // 2 % 2
                nc.vector.tensor_reduce(mxr[:, i - 1:i + 1], PS[:, 2 + 2 * pair:4 + 2 * pair, :], AX.X, ALU.max)\
                    .then_inc(max_done, 1)
                if i == 15:
                    s = 4 * b + g
                    dve.wait_ge(max_done, 8 * s + 8)
                    nc.vector.tensor_scalar(ms[:, 0, :].bitcast(F32R), mxr[:, :], -1.0, None, ALU.mult).then_inc(mh_done, 1)
                    dve.wait_ge(mh_done, s + 1)
                    nc.vector.scalar_tensor_tensor(ms[:, 1, :], mxr[:, :], -1.0, ms[:, 0, :], ALU.mult, ALU.subtract)\
                        .then_inc(ml_done, 1)
                    dve.wait_ge(ml_done, s + 1)

            def transpose_max(s, first=False):
                if not first:
                    dve.wait_ge(mscr_out, DMA * s)
                nc.vector.transpose(mT[:, :], ms[:, :, :].rearrange("p a k -> p (a k)")).then_inc(mt_ready, 1)

            for kk in range(1, AHEAD, 2):
                row_max(0, kk)
                if kk == 15:
                    transpose_max(0, True)

            def outputs(s, first=False):
                dve.wait_ge(av_done, 4 * s)
                nc.vector.transpose(OT[:, :, :].rearrange("p a c -> p (a c)"), OB).then_inc(ot_done, 1)
                dve.wait_ge(ot_done, s)
                nc.vector.reciprocal(rec[:, :], OT[:, :, HD]).then_inc(rec_done, 1)
                dve.wait_ge(rec_done, s)
                nc.vector.tensor_tensor(OTn[:, :, 0:HD], OT[:, :, 0:HD],
                                        rec[:, :].unsqueeze(2).broadcast_to([P, SEQ // 32, HD]), ALU.mult)\
                    .then_inc(otn_done, 1)
                dve.wait_ge(otn_done, s)
                dve.wait_ge(aol_done, s)
                nc.vector.transpose(AOf[:, :], OTn[:, :, :].rearrange("p a c -> p (a c)")).then_inc(aof_ready, 1)

            def add_attention(b, half):
                dve.wait_ge(wo_ready, 2 * b + half + 1)
                dve.wait_ge(bo_added, b + 1)
                v = X[:, bass.ds(TT * b + 2 * half, 2), :].rearrange("p t n -> p (t n)")
                nc.vector.tensor_tensor(v, v, MB, ALU.add).then_inc(x_done, 1)

            def slot(b, k, first, last):
                g, i = k // 16, k % 16
                kk = k + AHEAD
                if k % 2:
                    if kk < SLOTS:
                        row_max(b, kk)
                        if kk % 16 == 15:
                            transpose_max(4 * b + kk // 16)
                    elif not last:
                        row_max(b + 1, kk - SLOTS)
                        if kk % 16 == 15:
                            transpose_max(4 * b + kk // 16)
                if i == 4 and not (first and g == 0):
                    outputs(4 * b + g)
                if k in (12, 16) and not first:
                    add_attention(b - 1, (k - 12) // 4)
                if k == 17:
                    if last:
                        dve.wait_ge(x_done, 2 * b)
                        statistics(0, 0, TT, 3)
                    else:
                        normalise(TT * (b + 1), TT * (b + 1), b + 1)
                if k == 22 and last:
                    dve.wait_ge(rstd_done, 3)
                    normalise(0, 0, BATCH)

            def tail(b):
                outputs(4 * b)
                for half in range(2):
                    add_attention(b - 1, half)

            dve.wait_ge(rstd_done, 2)
            windows(dve, slot, tail)

            def prepare(n, X0):
                statistics(X0, 0, TT, n + 4)

            def ffn_chunk(n, f0, c4, X0, last):
                for f in range(FT):
                    dve.wait_ge(u_ready, FT * f0 + f + 1)
                    dve.wait_ge(sg_done, FT * f0 + f + 1)
                    nc.vector.tensor_tensor(PR[:, 2 + f % 2, :], PR[:, f % 2, :], PS[:, 2 + f % 2, :], ALU.mult)\
                        .then_inc(hf_done, 1)
                    dve.wait_ge(hh_done, FT * f0 + f + 1)
                    lo(AOl[:, f % 2, :], PR[:, 2 + f % 2, :], AOh[:, f % 2, :]).then_inc(hl_done, 1)
                    if f == 1 and not last:
                        dve.wait_ge(x_done, 2 * (n + BATCH))
                        pause()
                        prepare(n, X0)
                    if f == 3 and not last:
                        dve.wait_ge(rstd_done, n + 4)
                        normalise(X0, 0, n + BATCH + 1)
                add_output(n, c4, 4)

            def add_output(n, c4, bank):
                for half in range(2):
                    dve.wait_ge(y_ready, 2 * n + half + 1)
                    v = X[:, bass.ds(c4 + 2 * half, 2), :].rearrange("p t n -> p (t n)")
                    nc.vector.tensor_tensor(v, v, PS[:, bank + half, :], ALU.add).then_inc(x_done, 1)

            def mem_chunk(n, c4, X0):
                c0 = n - BATCH
                dve.wait_ge(x_done, 2 * (n + BATCH))
                pause()
                prepare(n, X0)
                for m in range(KD):
                    dve.wait_ge(bsg_done, KD * c0 + m + 1)
                    dve.wait_ge(bv_ready, KD * c0 + m + 1)
                    store, mem = PR[:, 4 + m, :], PR[:, 6 + m, :]
                    nc.vector.scalar_tensor_tensor(store, PS[:, 3 * m, :], MSCALE, PR[:, m, :], ALU.mult, ALU.mult)\
                        .then_inc(bst2_done, 1)
                    dve.wait_ge(bst2_done, KD * c0 + m + 1)
                    nc.vector.tensor_tensor_scan(mem, decay[:, 0:1].broadcast_to([P, SEQ]), store, 0.0, ALU.mult, ALU.add)\
                        .then_inc(scan_done, 1)
                    dve.wait_ge(scan_done, KD * c0 + m + 1)
                    dve.wait_ge(bsq_done, KD * c0 + m + 1)
                    nc.vector.scalar_tensor_tensor(store, mem, MSCALE, PR[:, 2 + m, :], ALU.mult, ALU.mult)\
                        .then_inc(load_done, 1)
                    if m == 0:
                        dve.wait_ge(rstd_done, n + 4)
                        normalise(X0, 0, n + BATCH + 1)
                    dve.wait_ge(lh_done, KD * c0 + m + 1)
                    lo(AOl[:, m, :], store, AOh[:, m, :]).then_inc(ll_done, 1)
                add_output(n, c4, 6)

            def following(i, cc):
                return TT * (2 * i + 1) if cc == 0 else 2 * TT * (1 - i)

            with dve.Fori(0, 2) as i:
                for cc in range(2):
                    ffn_chunk(2 * i + cc, 2 * i + cc, TT * (2 * i + cc), following(i, cc), False)
            with dve.Fori(0, 2) as i:
                for cc in range(2):
                    mem_chunk(BATCH + 2 * i + cc, TT * (2 * i + cc), following(i, cc))
            for c in range(BATCH):
                ffn_chunk(2 * BATCH + c, BATCH + c, TT * c, TT * ((c + 1) % BATCH), c == BATCH - 1)

        @block.gpsimd
        def _(pool):
            def reciprocal_deviation(n0, count, n):
                pool.wait_ge(mom_done, n)
                nc.gpsimd.tensor_tensor(veps[:, n0:n0 + count], mom[:, n0:n0 + count, 1], eps[:, n0:n0 + count], ALU.add)\
                    .then_inc(veps_done, 1)
                pool.wait_ge(veps_done, n)
                nc.gpsimd.tensor_tensor(rstd[:, n0:n0 + count], veps[:, n0:n0 + count], mhalf[:, n0:n0 + count], ALU.pow)\
                    .then_inc(rstd_done, 1)

            def lo(dst, src, h):
                return nc.gpsimd.tensor_tensor(dst, src, h.bitcast(F32), ALU.subtract)

            def x_lo_part(L, dt, par):
                pool.wait_ge(x_hi, 2 * L + dt + 1)
                lo(xTl[:, par, dt, :], xf[:, dt, :], xTh[:, par, dt, :]).then_inc(x_lo, 1)

            def qk_lo_part(b, n):
                pool.wait_ge(qk_hi, 4 * b + n + 1)
                lo(ql[:, n % 2, :], qf[:, n % 2, :], qh[:, n % 2, :]).then_inc(qk_lo, 1)

            def place_values(b, g, fresh=False):
                pool.wait_ge(v_copied, 2 * b + 2)
                if not fresh:
                    pool.wait_ge(av_done, 16 * b + 4 * g - 12)
                cs = slice(g * GH * HD, (g + 1) * GH * HD)
                nc.gpsimd.tensor_tensor(Vp[:, :, GH * g:GH * (g + 1), 0:HD],
                                        vst[:, :, cs].rearrange("p t (h c) -> p t h c", c=HD),
                                        bvt[:, cs].rearrange("p (h c) -> p h c", c=HD).unsqueeze(1)
                                        .broadcast_to([P, TT, GH, HD]), ALU.add).then_inc(vp_ready, 1)

            def output_lo(s, g):
                pool.wait_ge(aoh_done, s)
                lo(AOl[:, g, :], AOf[:, :], AOh[:, g, :]).then_inc(aol_done, 1)

            def add_bo(b):
                v = X[:, bass.ds(TT * b, TT), :]
                nc.gpsimd.tensor_tensor(v, v, bot[:, :].unsqueeze(1).broadcast_to([P, TT, D]), ALU.add).then_inc(bo_added, 1)

            nc.gpsimd.memset(mhalf[:, :], -0.5)
            nc.gpsimd.memset(eps[:, :], EPS).then_inc(pool_init, 1)
            nc.gpsimd.memset(Vp[:, :, :, HD:HD + 1], 1.0).then_inc(pool_init, 1)
            nc.gpsimd.memset(Vp[:, :, :, HD + 1:], 0.0).then_inc(hf_done, 2)
            pool.wait_ge(pool_init, 2)
            reciprocal_deviation(0, TT, 1)
            for dt in range(KD):
                x_lo_part(0, dt, 0)
            for n in range(4):
                qk_lo_part(0, n)
            for g in range(GROUPS):
                place_values(0, g, True)
            pool.wait_ge(xns_ready, 1)
            reciprocal_deviation(TT, (BATCH - 1) * TT, 2)
            add_bo(0)

            def slot(b, k, first, last):
                if k == 7 and not first:
                    output_lo(4 * b, GROUPS - 1)
                if k == 9 and not first:
                    place_values(b, GROUPS - 1)
                if k == 18 and not last:
                    pool.wait_ge(xns_ready, b + 2)
                    add_bo(b + 1)
                if k == 18 and last:
                    reciprocal_deviation(0, TT, 3)
                if k in ((26, 28) if last else (20, 22)):
                    x_lo_part(b + 1, 0 if k in (20, 26) else 1, 0)
                if k in (24, 40, 56):
                    output_lo(4 * b + k // 16, k // 16 - 1)
                if not last:
                    if k in (27, 29, 32, 35):
                        qk_lo_part(b + 1, (27, 29, 32, 35).index(k))
                    if k in (42, 43, 57):
                        place_values(b + 1, (42, 43, 57).index(k))

            nc.gpsimd.memset(credit[:, :], 0.0).then_inc(aol_done, 1)
            windows(pool, slot, lambda b: output_lo(4 * b, GROUPS - 1))

            def prepare(n, par):
                reciprocal_deviation(0, TT, n + 4)
                for dt in range(KD):
                    x_lo_part(n + BATCH + 1, dt, 1 - par)

            for n0 in (0, BATCH):
                with pool.Fori(0, 2) as i:
                    for cc in range(2):
                        prepare(n0 + 2 * i + cc, cc)
            for c in range(BATCH - 1):
                prepare(2 * BATCH + c, c % 2)


def kernel(**inputs):
    import numpy as np
    import concourse.bacc as bacc
    from concourse import mybir as mb
    from concourse.bass_utils import run_bass_kernel_spmd as run

    a = {k.split("_", 1)[1]: np.asarray(v) for k, v in inputs.items()}
    order = np.arange(D).reshape(2, HEADS // 2, HD).transpose(0, 2, 1).reshape(-1)
    wo = np.zeros((GROUPS, GH, 32, D), np.float32)
    wo[:, :, :HD, :] = a["attn_a_Wo"].T.reshape(GROUPS, GH, HD, D)
    bqk = np.stack([a["attn_a_bq"][order].reshape(KD, P), a["attn_a_bk"][order].reshape(KD, P)], 1).reshape(2 * KD, P).T
    bgq = np.concatenate([a["attn_b_bg"].reshape(KD, P), a["attn_b_bq"].reshape(KD, P)]).T
    had = np.ones((1, 1), np.float32)
    while had.shape[0] < P:
        had = np.block([[had, had], [had, -had]])
    arrays = {
        "x": a["attn_a_x"], "wq": a["attn_a_Wq"].T[:, order], "wk": a["attn_a_Wk"].T[:, order],
        "wv": a["attn_a_Wv"].T, "wo": wo.reshape(GROUPS, P, D), "bqk_d": bqk, "bgq_d": bgq, "bv": a["attn_a_bv"], "bo": a["attn_a_bo"],
        "mv_": a["attn_b_Wv"], "mg": a["attn_b_Wg"], "mq": a["attn_b_Wq"], "mo": a["attn_b_Wo"], "w1": a["ffn_W1"].T, "w2": a["ffn_W2"].T,
        "w3": a["ffn_W3"].T, "ident_d": np.eye(P, dtype=np.float32), "had_d": had.astype(np.float32),
    }
    arrays = {k: np.ascontiguousarray(v) for k, v in arrays.items()}
    nc = bacc.Bacc("TRN2", target_bir_lowering=False, num_devices=1)
    args = {k: nc.dram_tensor(f"in_{k}", v.shape, mb.dt.from_np(v.dtype), kind="ExternalInput").ap()
            for k, v in arrays.items()}
    args["out"] = nc.dram_tensor("out_0", [BATCH, SEQ, D], F32, kind="ExternalOutput").ap()
    build(nc, **args)
    got = run(nc, [{f"in_{k}": v for k, v in arrays.items()}], core_ids=[0])
    return got.results[0]["out_0"]
```

```python
from contextlib import ExitStack

import concourse.bass as bass
from concourse import mybir

F32 = mybir.dt.float32
F32R = mybir.dt.float32r
ALU = mybir.AluOpType
ACT = mybir.ActivationFunctionType
AX = mybir.AxisListType

P = 128
BATCH, SEQ, D = 4, 512, 256
HEADS, HD = 16, 16
HID = 1024
TT = SEQ // P
KD = D // P
GROUPS = 4
GH = HEADS // GROUPS
FT = HID // P
SLOTS = GROUPS * TT * GH
AHEAD = 24
TURN = 18
OUT_PE, OUT_ADD = (8, 13), (12, 17)
LN_PE = (20, 22)
QK_PE, QK_OUT, RING_IN = (25, 29, 33, 37), (29, 33, 37, 41), (34, 38, 49)
V_PE, V_PLACE = (41, 45), (48, 49, 57)
SPLIT_AT = (31, 33, 35, 37, 42, 44, 46, 48, 57, 59, 61, 63)
QROWS = 4 * HD
MROW = 96
DMA = 16
EPS = 1e-5
DECAY = 0.95
MSCALE = float((1.0 - DECAY) ** 0.5)
QI, KI = 0, 1


def build(nc, x, wq, wk, wv, wo, bqk_d, bv, bo, mv_, mg, mq, bgq_d, mo, w1, w2, w3, ident_d, had_d, out):
    ctx = ExitStack()
    with ctx:
        def sb(name, shape, dt=F32):
            return ctx.enter_context(nc.sbuf_tensor(name, shape, dt))

        def sem(name):
            return ctx.enter_context(nc.semaphore(name))

        X = sb("X", [P, BATCH * TT, D])
        XNs = sb("XNs", [P, TT, D])
        xf = sb("xf", [P, KD, SEQ])
        xTh = sb("xTh", [P, 2, KD, SEQ], F32R)
        xTl = sb("xTl", [P, 2, KD, SEQ], F32R)
        ring = sb("ring", [P, GROUPS, 2, GH, SEQ], F32R)
        PR = sb("PR", [P, 8, SEQ])
        Vp = sb("Vp", [P, TT, HEADS, 2 * HD])
        vst = sb("vst", [P, TT, D])
        qf = sb("qf", [P, 2, SEQ])
        qh = sb("qh", [P, 2, SEQ], F32R)
        ql = sb("ql", [P, 2, SEQ], F32R)
        OT = sb("OT", [P, SEQ // 32, 32])
        OTn = sb("OTn", [P, SEQ // 32, 32])
        AOf = sb("AOf", [P, SEQ])
        AOh = sb("AOh", [P, GROUPS, SEQ], F32R)
        AOl = sb("AOl", [P, GROUPS, SEQ], F32R)
        WAh = sb("WAh", [P, 3, KD, D], F32R)
        WAl = sb("WAl", [P, 3, KD, D], F32R)
        WOh = sb("WOh", [P, GROUPS, D], F32R)
        WOl = sb("WOl", [P, GROUPS, D], F32R)
        bqk = sb("bqk", [P, 4])
        bgq = sb("bgq", [P, 4])
        bvt = sb("bvt", [P, D])
        bot = sb("bot", [P, D])
        ident = sb("ident", [P, P])
        had = sb("had", [P, P])
        mxr = sb("mxr", [P, GH * TT])
        ms = sb("ms", [P, 2, GH * TT])
        mT = sb("mT", [P, 32])
        rec = sb("rec", [P, SEQ // 32])
        bst = sb("bst", [P, BATCH * TT, 6])
        mom = sb("mom", [P, BATCH * TT, 2])
        veps = sb("veps", [P, BATCH * TT])
        rstd = sb("rstd", [P, BATCH * TT])
        eps = sb("eps", [P, BATCH * TT])
        mhalf = sb("mhalf", [P, BATCH * TT])
        decay = sb("decay", [P, 1])
        spare = sb("spare", [P, 1])
        credit = sb("credit", [P, 1])
        PS = ctx.enter_context(nc.psum_tensor("PS", [P, 8, SEQ], F32))
        OB, MB = PS[:, 6, :], PS[:, 7, :]
        qscr = nc.dram_tensor("qk_scratch", [BATCH, 2, 2, 2, HD, HEADS // 2, SEQ], F32, kind="Internal").ap()
        mscr = nc.dram_tensor("max_scratch", [GROUPS, 2 * GH * TT, P // 32, 32], F32, kind="Internal").ap()
        wscr = nc.dram_tensor("weight_scratch", [4, P, KD * HID], F32, kind="Internal").ap()
        W_UP, W_LIN, W_DOWN, W_MEM = range(4)

        def parts(slot):
            v = ring[:, slot, :, :, :].rearrange("p a h n -> p a (h n)")
            return v[:, 0, :], v[:, 1, :]

        def quarter(slot, i):
            return tuple(v[:, i * SEQ:(i + 1) * SEQ] for v in parts(slot))

        x_in = [sem(f"x_in{b}") for b in range(BATCH)]
        wqk_in, wv_in, wo_in, bias_in, ident_in, const_in = (sem(n) for n in ("wqk_in", "wv_in", "wo_in", "bias_in",
                                                                          "ident_in", "const_in"))
        w2_in = sem("w2_in")
        zero_done, one_done, pool_init, fill_in, whi_done, wlo_done, had_ready, had_copied, fly_done = (
            sem(n) for n in ("zero_done", "one_done", "pool_init", "fill_in", "whi_done", "wlo_done", "had_ready",
                             "had_copied", "fly_done"))
        bst_done, mom_done, veps_done, rstd_done, xns_ready, lnT_ready, x_f, x_hi, x_lo = (
            sem(n) for n in ("bst_done", "mom_done", "veps_done", "rstd_done", "xns_ready", "lnT_ready", "x_f", "x_hi",
                             "x_lo"))
        qk_ready, qk_f, qk_hi, qk_lo, v_ready, v_copied, vp_ready, bo_added = (
            sem(n) for n in ("qk_ready", "qk_f", "qk_hi", "qk_lo", "v_ready", "v_copied", "vp_ready", "bo_added"))
        scr_out = [sem("scr_out0"), sem("scr_out1")]
        ring_in = [sem(f"ring_in{g}") for g in range(GROUPS)]
        s1_ready, max_done, mh_done, ml_done, mt_ready, mscr_out = (
            sem(n) for n in ("s1_ready", "max_done", "mh_done", "ml_done", "mt_ready", "mscr_out"))
        mrow_in = [sem(f"mrow_in{g}") for g in range(GROUPS)]
        st_ready, exp_done, av_done, ot_done, rec_done, otn_done, aof_ready, aoh_done, aol_done, wo_ready, x_done = (
            sem(n) for n in ("st_ready", "exp_done", "av_done", "ot_done", "rec_done", "otn_done", "aof_ready",
                             "aoh_done", "aol_done", "wo_ready", "x_done"))
        scr_w = [sem(f"scr_w{g}") for g in range(4)]
        w_in = [sem(f"w_in{g}") for g in range(4)]
        lhi_done, llo_done, mem_hi, mem_lo = (sem(n) for n in ("lhi_done", "llo_done", "mem_hi", "mem_lo"))
        g_ready, u_ready, sg_done, hf_done, hh_done, hl_done, y_ready = (
            sem(n) for n in ("g_ready", "u_ready", "sg_done", "hf_done", "hh_done", "hl_done", "y_ready"))
        bg_ready, bq_ready, bv_ready, bsg_done, bsq_done, bst2_done, scan_done, load_done, lh_done, ll_done = (
            sem(n) for n in ("bg_ready", "bq_ready", "bv_ready", "bsg_done", "bsq_done", "bst2_done", "scan_done",
                             "load_done", "lh_done", "ll_done"))
        out_done = sem("out_done")

        def windows(eng, slot, tail):
            for k in range(TURN):
                slot(0, k, True, False)
            with eng.Fori(0, BATCH - 1) as b:
                for k in range(TURN, SLOTS):
                    slot(b, k, False, False)
                for k in range(TURN):
                    slot(b + 1, k, False, False)
            for k in range(TURN, SLOTS):
                slot(BATCH - 1, k, False, True)
            tail(BATCH)

        block = ctx.enter_context(nc.Block())

        @block.sync
        def _(sp):
            xv = x.rearrange("b (t p) d -> b p t d", p=P)
            sp.dma_start(X[:, 0:TT, :], xv[0, :, :, :]).then_inc(x_in[0], DMA)
            for i, w in enumerate((wq, wk)):
                sp.dma_start(qf[:, i, :].rearrange("p (k n) -> p k n", k=KD),
                             w.rearrange("(k p) n -> p k n", p=P)).then_inc(wqk_in, DMA)
            sp.dma_start(xf[:, 0, :].rearrange("p (k n) -> p k n", k=KD),
                         wv.rearrange("(k p) n -> p k n", p=P)).then_inc(wv_in, DMA)
            sp.dma_start(ident[:, :], ident_d).then_inc(ident_in, DMA)
            sp.dma_start(bqk[:, :], bqk_d).then_inc(bias_in, DMA)
            sp.dma_start(PR[:, 0:4, :].rearrange("p a (u n) -> p (a u) n", n=D),
                         w2.rearrange("(f p) n -> p f n", p=P)).then_inc(w2_in, DMA)
            sp.dma_start(had[:, :], had_d).then_inc(w2_in, DMA)
            sp.dma_start(vst[:, :, :], wo.rearrange("g p n -> p g n")).then_inc(wo_in, DMA)
            sp.dma_start(bvt[:, :], bv.partition_broadcast(P)).then_inc(const_in, DMA)
            sp.dma_start(bot[:, :], bo.partition_broadcast(P)).then_inc(const_in, DMA)
            sp.dma_start(bgq[:, :], bgq_d).then_inc(const_in, DMA)
            sp.wait_ge(zero_done, 1)
            sp.dma_start(ring[QROWS:MROW, :, :, :, :].rearrange("p g a h n -> p (g a h) n").bitcast(F32),
                         OTn[0:MROW - QROWS, :, :].rearrange("p a c -> p (a c)").unsqueeze(1)
                         .broadcast_to([MROW - QROWS, GROUPS * 2 * GH, SEQ])).then_inc(fill_in, DMA)
            sp.wait_ge(one_done, 1)
            for g in range(GROUPS):
                sp.dma_start(ring[MROW:MROW + 2, g, KI, :, :].bitcast(F32),
                             AOf[0:2, :].unsqueeze(1).broadcast_to([2, GH, SEQ])).then_inc(fill_in, DMA)
            for b in range(1, BATCH):
                sp.dma_start(X[:, b * TT:(b + 1) * TT, :], xv[b, :, :, :]).then_inc(x_in[b], DMA)

            def scratch_out(b, n):
                sp.wait_ge(qk_lo, 4 * b + n + 1)
                mt, qk = n // 2, n % 2
                for part, t in ((0, qh), (1, ql)):
                    sp.dma_start(qscr[b, qk, part, mt, :, :, :].rearrange("r h n -> (r h) n"),
                                 t[:, n % 2, :].bitcast(F32)).then_inc(scr_out[n % 2], DMA)

            def ring_load(b, g):
                mt, h0 = g // 2, GH * (g % 2)
                for qk in (QI, KI):
                    sp.wait_ge(scr_out[qk], 2 * DMA * (2 * b + mt + 1))
                    for a in range(2):
                        dst = ring[32 * a:32 * a + 32, g, qk, :, :].rearrange("p h n -> p (h n)").bitcast(F32)
                        if qk == QI:
                            src = qscr[b, qk, a, mt, :, h0:h0 + GH, :].rearrange("r h n -> r (h n)")
                            src = src.unsqueeze(0).broadcast_to([2, HD, GH * SEQ])
                        else:
                            src = qscr[b, qk, :, mt, :, h0:h0 + GH, :].rearrange("a r h n -> a r (h n)")
                        sp.dma_start(dst, src).then_inc(ring_in[g], DMA)

            def max_rows(b, g):
                sp.wait_ge(mt_ready, 4 * b + g + 1)
                sp.dma_start(mscr[g, :, :, :].rearrange("k c n -> c k n"), mT[:, :]).then_inc(mscr_out, DMA)
                sp.wait_ge(mscr_out, DMA * (4 * b + g + 1))
                sp.dma_start(ring[MROW:MROW + 2, g, QI, :, :].rearrange("p h n -> p (h n)").bitcast(F32),
                             mscr[g, :, :, :].rearrange("(a k) c n -> a (k c n)", a=2)).then_inc(mrow_in[g], DMA)

            def weights_in(w):
                sp.wait_ge(st_ready, SLOTS * (BATCH - 1) + 16 * (w + 1))
                sp.wait_ge(scr_w[w], (4 if w == W_MEM else 1) * DMA)
                sp.dma_start(parts(w)[1].bitcast(F32), wscr[w, :, :]).then_inc(w_in[w], DMA)

            def layout(w, j, k, src):
                sp.dma_start(wscr[w, :, j * SEQ:(j + k) * SEQ].rearrange("p (k n) -> p k n", k=KD),
                             src.rearrange("(k p) n -> p k n", p=P)).then_inc(scr_w[w], DMA)

            for n in range(2):
                scratch_out(0, n)
            ring_load(0, 0)
            ring_load(0, 1)
            for n in range(2, 4):
                scratch_out(0, n)
            ring_load(0, 2)
            ring_load(0, 3)
            sp.wait_ge(fly_done, 3)
            sp.dma_start(wscr[W_DOWN, :, :], PR[:, 4:8, :].rearrange("p a n -> p (a n)")).then_inc(scr_w[W_DOWN], DMA)
            layout(W_UP, 0, 4, w1)
            layout(W_LIN, 0, 4, w3)
            for j, src in enumerate((mv_, mg, mq, mo)):
                layout(W_MEM, j, 1, src)
            max_rows(0, 0)

            def slot(b, k, first, last):
                g, i = k // 16, k % 16
                if k == 1 and not first:
                    sp.wait_ge(st_ready, SLOTS * b)
                    ring_load(b, 3)
                if i == 9 and not (last and g == 3):
                    max_rows(b + (g + 1) // GROUPS, (g + 1) % GROUPS)
                if not last:
                    if k in QK_OUT:
                        scratch_out(b + 1, QK_OUT.index(k))
                    if k in RING_IN:
                        g1 = RING_IN.index(k)
                        sp.wait_ge(st_ready, SLOTS * b + 16 * (g1 + 1))
                        ring_load(b + 1, g1)
                elif k in (18, 33, 49):
                    weights_in(g - 1)

            windows(sp, slot, lambda b: weights_in(W_MEM))
            ov = out.rearrange("b (t p) d -> b p t d", p=P)
            for c in range(BATCH):
                sp.wait_ge(x_done, 2 * (BATCH + 2 * BATCH + c + 1))
                sp.dma_start(ov[c, :, :, :], X[:, c * TT:(c + 1) * TT, :]).then_inc(out_done, DMA)
            sp.wait_ge(out_done, DMA * BATCH)

        @block.tensor
        def _(pe):
            def mm(dst, lhsT, rhs, start, stop):
                return nc.tensor.matmul(dst, lhsT, rhs, start=start, stop=stop, skip_group_check=True)

            def split_mm(dst, pairs, start=True, stop=True):
                n = 3 * len(pairs)
                ops = [(l, r) for ll, lh, rl, rh in pairs for l, r in ((ll, rh), (lh, rl), (lh, rh))]
                for i, (l, r) in enumerate(ops):
                    last = mm(dst, l, r, start and i == 0, stop and i == n - 1)
                return last

            def ln_transpose(L, dt, bank):
                for t in range(TT):
                    last = nc.tensor.transpose(bank[:, t * P:(t + 1) * P], XNs[:, t, dt * P:(dt + 1) * P], ident[:, :])
                last.then_inc(lnT_ready, 1)

            def xt(par, kt):
                return xTl[:, par, kt, :], xTh[:, par, kt, :]

            def project_qk(b, n, part, bank=MB):
                w, m = n % 2, n // 2 * P
                ops = [(lo, r, kt) for kt in range(KD) for lo, r in ((1, 1), (0, 0), (0, 1))]
                for i in (2 * part, 2 * part + 1):
                    lo, r, kt = ops[i]
                    lhsT = (WAl if lo else WAh)[:, w, kt, m:m + P]
                    last = mm(bank, lhsT, xt(0, kt)[r], i == 0, i == 5)
                if part == 2:
                    last.then_inc(qk_ready, 1)

            def project_v(b, half, part, bank=MB):
                ops = [(t, kt, l, w) for t in range(2) for kt in range(KD) for l, w in ((0, WAh), (1, WAl), (1, WAh))]
                for i in range(4 * part, 4 * part + 4):
                    t, kt, l, w = ops[i]
                    tok = (2 * half + t) * P
                    last = mm(bank[:, t * D:(t + 1) * D], xt(0, kt)[l][:, tok:tok + P], w[:, 2, kt, :],
                              i % 6 == 0, i % 6 == 5)
                if part == 2:
                    last.then_inc(v_ready, 1)

            def out_projection(b, half, part):
                ops = [(t, g, a, w) for t in range(2) for g in range(GROUPS)
                       for a, w in ((AOl, WOh), (AOh, WOl), (AOh, WOh))]
                for i in range(6 * part, 6 * part + 6):
                    t, g, a, w = ops[i]
                    tok = (2 * half + t) * P
                    last = mm(MB[:, t * D:(t + 1) * D], a[:, g, tok:tok + P], w[:, g, :], i % 12 == 0, i % 12 == 11)
                if part == 3:
                    last.then_inc(wo_ready, 1)

            def score_qk(b, kk, fresh=False):
                g, i = kk // 16, kk % 16
                j, t, pair = i // TT, i % TT, kk // 2 % 2
                if i == 0:
                    pe.wait_ge(ring_in[g], 4 * DMA * (b + 1))
                if kk % 2 == 0 and not (fresh and kk < 4):
                    pe.wait_ge(max_done, 32 * b + kk // 2 - 1)
                last = mm(PS[:, 2 + 2 * pair + t % 2, :], ring[0:MROW, g, QI, j, t * P:(t + 1) * P],
                          ring[0:MROW, g, KI, j, :], True, True)
                if kk % 2:
                    last.then_inc(s1_ready, 1)

            def score_kq(b, k, first):
                g, i = k // 16, k % 16
                kt, j = i // GH, i % GH
                if i == 0:
                    pe.wait_ge(mrow_in[g], DMA * (b + 1))
                if not (first and k < 2):
                    pe.wait_ge(exp_done, SLOTS * b + k - 1)
                mm(PS[:, k % 2, :], ring[0:MROW + 2, g, KI, j, kt * P:(kt + 1) * P], ring[0:MROW + 2, g, QI, j, :],
                   True, True).then_inc(st_ready, 1)

            def weigh_values(b, g, kt, first=False):
                s = 4 * b + g
                pe.wait_ge(exp_done, 16 * s + 4 * kt + 4)
                if kt == 0:
                    pe.wait_ge(vp_ready, s + 1)
                    if not first:
                        pe.wait_ge(ot_done, s)
                for j in range(GH):
                    last = mm(OB[32 * j:32 * j + 32, :], Vp[:, kt, GH * g + j, :], PR[:, (4 * kt + j) % 8, :],
                              kt == 0, kt == TT - 1)
                last.then_inc(av_done, 1)

            pe.wait_ge(ident_in, DMA)
            pe.wait_ge(xns_ready, 1)
            for dt in range(KD):
                ln_transpose(0, dt, PS[:, dt, :])
            pe.wait_ge(wlo_done, 3)
            pe.wait_ge(x_lo, 2)
            for n in range(4):
                for part in range(3):
                    project_qk(0, n, part, PS[:, 2 + n, :])
            pe.wait_ge(w2_in, 2 * DMA)
            pe.wait_ge(qk_f, 2)
            for n in range(FT // 2):
                last = mm(PS[:, n, :], had[:, :], PR[:, n, :], True, True)
            last.then_inc(had_ready, 1)
            for half in range(2):
                for part in range(3):
                    project_v(0, half, part, PS[:, 6 + half, :])
            pe.wait_ge(fill_in, (1 + GROUPS) * DMA)
            pe.wait_ge(had_copied, 1)
            pe.wait_ge(v_copied, 2)
            for kk in range(AHEAD):
                score_qk(0, kk, True)

            def slot(b, k, first, last):
                g, i = k // 16, k % 16
                score_kq(b, k, first)
                kk = k + AHEAD
                if kk < SLOTS:
                    score_qk(b, kk)
                elif not last:
                    score_qk(b + 1, kk - SLOTS)
                if i % 4 == 2:
                    if i > 2:
                        weigh_values(b, g, i // 4 - 1, first and g == 0)
                    elif g:
                        weigh_values(b, g - 1, TT - 1)
                    elif not first:
                        weigh_values(b - 1, GROUPS - 1, TT - 1)
                if not first and (OUT_PE[0] <= k < OUT_PE[0] + 4 or OUT_PE[1] <= k < OUT_PE[1] + 4):
                    if k == OUT_PE[0]:
                        pe.wait_ge(aol_done, 4 * b + 1)
                        pe.wait_ge(v_copied, 2 * b + 2)
                    half = int(k >= OUT_PE[1])
                    if k == OUT_PE[1]:
                        pe.wait_ge(x_done, 2 * b - 1)
                    out_projection(b - 1, half, k - OUT_PE[half])
                if k == LN_PE[0] + 6 * last:
                    pe.wait_ge(xns_ready, b + 2)
                    ln_transpose(b + 1, 0, MB)
                if k == LN_PE[1] + 6 * last:
                    pe.wait_ge(x_f, 2 * b + 3)
                    ln_transpose(b + 1, 1, MB)
                if not last:
                    for n, k0 in enumerate(QK_PE):
                        if k == k0 and n == 0:
                            pe.wait_ge(x_lo, 2 * b + 4)
                        elif k == k0:
                            pe.wait_ge(qk_f, 4 * b + 4 + n)
                        if k0 <= k < k0 + 3:
                            project_qk(b + 1, n, k - k0)
                    for half, k0 in enumerate(V_PE):
                        if k == k0 and half == 0:
                            pe.wait_ge(qk_f, 4 * b + 8)
                        elif k == k0:
                            pe.wait_ge(v_copied, 2 * b + 3)
                        if k0 <= k < k0 + 3:
                            project_v(b + 1, half, k - k0)

            def tail(b):
                weigh_values(b - 1, GROUPS - 1, TT - 1)
                pe.wait_ge(x_f, 2 * b + 2)
                pe.wait_ge(max_done, 8 * GROUPS * b)
                for g in range(GROUPS):
                    if g in (0, GROUPS - 1):
                        pe.wait_ge(aol_done, 4 * b + (g > 0))
                    for t in range(TT):
                        ts = slice(t * P, (t + 1) * P)
                        last = split_mm(PS[:, (7, 5)[t // 2], t % 2 * D:(t % 2 + 1) * D],
                                        [(AOl[:, g, ts], AOh[:, g, ts], WOl[:, g, :], WOh[:, g, :])],
                                        g == 0 and t % 2 == 0, g == GROUPS - 1)
                        if g == GROUPS - 1 and t % 2:
                            last.then_inc(wo_ready, 1)

            windows(pe, slot, tail)

            def ffn_chunk(p, n, f0, par, last):
                w1h, w1l = (v.rearrange("p (k n) -> p k n", k=KD) for v in parts(W_UP))
                w3h, w3l = (v.rearrange("p (k n) -> p k n", k=KD) for v in parts(W_LIN))
                w2h, w2l = (v.rearrange("p (f n) -> p f n", f=FT) for v in parts(W_DOWN))

                def down(f):
                    pe.wait_ge(hl_done, FT * f0 + f + 1)
                    for t in range(TT):
                        ts = slice(t * P, (t + 1) * P)
                        last_ = split_mm(PS[:, 4 + t // 2, t % 2 * D:(t % 2 + 1) * D],
                                         [(AOl[:, f % 2, ts], AOh[:, f % 2, ts], w2l[:, f, :], w2h[:, f, :])],
                                         f == 0 and t % 2 == 0, f == FT - 1)
                        if f == FT - 1 and t % 2:
                            last_.then_inc(y_ready, 1)

                pe.wait_ge(x_lo, 2 * (n + BATCH + 1))
                for f in range(FT):
                    fs = slice(f * P, (f + 1) * P)
                    pe.wait_ge(hf_done, FT * f0 + f + 1)
                    for bank, wl, wh, ready in ((f % 2, w1l, w1h, g_ready), (2 + f % 2, w3l, w3h, u_ready)):
                        split_mm(PS[:, bank, :], [(wl[:, k, fs], wh[:, k, fs]) + xt(par, k) for k in range(KD)])\
                            .then_inc(ready, 1)
                    if f == 1:
                        pe.wait_ge(x_done, 2 * (n + BATCH))
                    if f:
                        down(f - 1)
                    if f == 4 and not last:
                        pe.wait_ge(xns_ready, n + BATCH + 2)
                        ln_transpose(n + 1, 0, PS[:, 6, :])
                        ln_transpose(n + 1, 1, PS[:, 7, :])
                down(FT - 1)

            def mem_chunk(n, par):
                wh, wl = (v.rearrange("p (w k n) -> p w k n", w=4, k=KD) for v in parts(W_MEM))
                c0 = n - BATCH
                pe.wait_ge(x_lo, 2 * (n + BATCH + 1))
                for m in range(KD):
                    if m:
                        pe.wait_ge(x_done, 2 * (n + BATCH))
                    ms_ = slice(m * P, (m + 1) * P)
                    for w, ready in ((1, bg_ready), (2, bq_ready), (0, bv_ready)):
                        split_mm(PS[:, 3 * m + w, :],
                                 [(wl[:, w, k, ms_], wh[:, w, k, ms_]) + xt(par, k) for k in range(KD)])\
                            .then_inc(ready, 1)
                pe.wait_ge(xns_ready, n + BATCH + 2)
                for dt in range(KD):
                    ln_transpose(n + 1, dt, PS[:, 6 + dt, :])
                pe.wait_ge(x_f, 2 * (n + BATCH + 2))
                for m in range(KD):
                    pe.wait_ge(ll_done, KD * c0 + m + 1)
                    for t in range(TT):
                        ts = slice(t * P, (t + 1) * P)
                        last = split_mm(PS[:, 6 + t // 2, t % 2 * D:(t % 2 + 1) * D],
                                        [(AOl[:, m, ts], AOh[:, m, ts], wl[:, 3, m, :], wh[:, 3, m, :])],
                                        m == 0 and t % 2 == 0, m == KD - 1)
                        if m == KD - 1 and t % 2:
                            last.then_inc(y_ready, 1)

            pe.wait_ge(llo_done, 3 * 4)
            with pe.Fori(0, 2) as i:
                for cc in range(2):
                    ffn_chunk(0, 2 * i + cc, 2 * i + cc, cc, False)
            pe.wait_ge(mem_lo, 4)
            with pe.Fori(0, 2) as i:
                for cc in range(2):
                    mem_chunk(BATCH + 2 * i + cc, cc)
            for c in range(BATCH):
                ffn_chunk(2, 2 * BATCH + c, BATCH + c, c % 2, c == BATCH - 1)

        @block.scalar
        def _(act):
            def hi(dst, src, scale=1.0):
                return nc.scalar.activation(dst, src, ACT.Copy, scale=scale)

            def ln_evacuate(L, dt, bank, fresh=False):
                act.wait_ge(lnT_ready, 2 * L + dt + 1)
                if not fresh:
                    act.wait_ge(x_lo, 2 * L - 1 + dt)
                hi(xf[:, dt, :], bank).then_inc(x_f, 1)

            def ln_hi(L, dt, par):
                act.wait_ge(x_f, 2 * L + dt + 1)
                hi(xTh[:, par, dt, :], xf[:, dt, :]).then_inc(x_hi, 1)

            def qk_evacuate(b, n, bank=MB, fresh=False):
                act.wait_ge(qk_ready, 4 * b + n + 1)
                if not fresh:
                    act.wait_ge(qk_lo, 4 * b + n - 1)
                nc.scalar.activation(qf[:, n % 2, :], bank, ACT.Identity, bias=bqk[:, n:n + 1]).then_inc(qk_f, 1)

            def qk_split(b, n, fresh=False):
                act.wait_ge(qk_f, 4 * b + n + 1)
                if not fresh:
                    act.wait_ge(scr_out[n % 2], 2 * DMA * (2 * b + n // 2))
                hi(qh[:, n % 2, :], qf[:, n % 2, :]).then_inc(qk_hi, 1)

            def v_evacuate(b, half, bank=MB, fresh=False):
                act.wait_ge(v_ready, 2 * b + half + 1)
                if not fresh:
                    act.wait_ge(vp_ready, 4 * b)
                hi(vst[:, 2 * half:2 * half + 2, :].rearrange("p t n -> p (t n)"), bank).then_inc(v_copied, 1)

            act.wait_ge(wqk_in, 2 * DMA)
            for i in range(2):
                hi(WAh[:, i, :, :].rearrange("p k n -> p (k n)"), qf[:, i, :]).then_inc(whi_done, 1)
            act.wait_ge(wv_in, DMA)
            hi(WAh[:, 2, :, :].rearrange("p k n -> p (k n)"), xf[:, 0, :]).then_inc(whi_done, 1)
            act.wait_ge(wlo_done, 3)
            for dt in range(KD):
                ln_evacuate(0, dt, PS[:, dt, :], True)
                ln_hi(0, dt, 0)
            act.wait_ge(bias_in, DMA)
            for n in range(4):
                qk_evacuate(0, n, PS[:, 2 + n, :], n < 2)
                qk_split(0, n, n < 2)
            act.wait_ge(wo_in, DMA)
            hi(WOh[:, :, :].rearrange("p g n -> p (g n)"), vst[:, :, :].rearrange("p t n -> p (t n)")).then_inc(whi_done, 1)
            act.wait_ge(had_ready, 1)
            for n in range(FT // 2):
                last = hi(PR[:, n, :], PS[:, n, :], 1.0 / HID ** 0.5)
            last.then_inc(had_copied, 1)
            act.wait_ge(wlo_done, 4)
            for half in range(2):
                v_evacuate(0, half, PS[:, 6 + half, :], True)
            act.wait_ge(fly_done, 3)

            def w_hi(w, i):
                if i == 0:
                    act.wait_ge(w_in[w], DMA)
                h, raw = quarter(w, i)
                hi(h, raw.bitcast(F32)).then_inc(lhi_done, 1)

            def slot(b, k, first, last):
                g, i = k // 16, k % 16
                act.wait_ge(st_ready, SLOTS * b + k + 1)
                if k % 4 == 0 and not (first and k < 8):
                    act.wait_ge(av_done, 16 * b + k // 4 - 1)
                if k == 4 and first:
                    act.wait_ge(scr_w[W_DOWN], DMA)
                nc.scalar.activation(PR[:, k % 8, :], PS[:, k % 2, :], ACT.Exp, scale=HD ** -0.5).then_inc(exp_done, 1)
                if i == 6 and not (first and g == 0):
                    act.wait_ge(aof_ready, 4 * b + g)
                    hi(AOh[:, (g - 1) % GROUPS, :], AOf[:, :]).then_inc(aoh_done, 1)
                for dt in range(KD):
                    if k == LN_PE[dt] + 6 * last:
                        ln_evacuate(b + 1, dt, MB)
                    if k == LN_PE[dt] + 6 * last + 1:
                        ln_hi(b + 1, dt, 0)
                if not last:
                    for n, k0 in enumerate(QK_PE):
                        if k == k0 + 2:
                            qk_evacuate(b + 1, n)
                        if k == k0 + 3:
                            qk_split(b + 1, n)
                    if k - 2 in V_PE:
                        v_evacuate(b + 1, V_PE.index(k - 2))
                elif k in SPLIT_AT:
                    n = SPLIT_AT.index(k)
                    w_hi(n // 4, n % 4)

            def tail(b):
                act.wait_ge(aof_ready, 4 * b)
                hi(AOh[:, GROUPS - 1, :], AOf[:, :]).then_inc(aoh_done, 1)

            windows(act, slot, tail)

            def ffn_chunk(n, f0, par, last):
                for f in range(FT):
                    act.wait_ge(g_ready, FT * f0 + f + 1)
                    nc.scalar.activation(PR[:, f % 2, :], PS[:, f % 2, :], ACT.Silu).then_inc(sg_done, 1)
                    act.wait_ge(hf_done, FT * f0 + f + 3)
                    hi(AOh[:, f % 2, :], PR[:, 2 + f % 2, :]).then_inc(hh_done, 1)
                    if f == 5 and not last:
                        for dt in range(KD):
                            ln_evacuate(n + BATCH + 1, dt, PS[:, 6 + dt, :])
                            ln_hi(n + BATCH + 1, dt, 1 - par)

            def mem_chunk(n, par):
                c0 = n - BATCH
                for m in range(KD):
                    act.wait_ge(bg_ready, KD * c0 + m + 1)
                    nc.scalar.activation(PR[:, m, :], PS[:, 3 * m + 1, :], ACT.Sigmoid, bias=bgq[:, m:m + 1]).then_inc(bsg_done, 1)
                    act.wait_ge(bq_ready, KD * c0 + m + 1)
                    nc.scalar.activation(PR[:, 2 + m, :], PS[:, 3 * m + 2, :], ACT.Sigmoid, bias=bgq[:, 2 + m:3 + m]).then_inc(bsq_done, 1)
                    if m:
                        for dt in range(KD):
                            ln_evacuate(n + BATCH + 1, dt, PS[:, 6 + dt, :])
                            ln_hi(n + BATCH + 1, dt, 1 - par)
                    act.wait_ge(load_done, KD * c0 + m + 1)
                    hi(AOh[:, m, :], PR[:, 4 + m, :]).then_inc(lh_done, 1)

            with act.Fori(0, 2) as i:
                for cc in range(2):
                    ffn_chunk(2 * i + cc, 2 * i + cc, cc, False)
            with act.Fori(0, 2) as i:
                for cc in range(2):
                    mem_chunk(BATCH + 2 * i + cc, cc)
            for c in range(BATCH):
                ffn_chunk(2 * BATCH + c, BATCH + c, c % 2, c == BATCH - 1)

        @block.vector
        def _(dve):
            def pause():
                nc.vector.memset(spare[:, :], 0.0)

            def statistics(X0, n0, count, n):
                for t in range(count):
                    last = nc.vector.bn_stats(bst[:, n0 + t, :], X[:, X0 + t, :])
                last.then_inc(bst_done, 1)
                dve.wait_ge(bst_done, n)
                pause()
                for t in range(count):
                    last = nc.vector.bn_aggr(mom[:, n0 + t, :], bst[:, n0 + t, :])
                last.then_inc(mom_done, 1)

            def normalise(X0, n0, L, fresh=False):
                if not fresh:
                    dve.wait_ge(lnT_ready, 2 * L)
                for t in range(TT):
                    last = nc.vector.tensor_scalar(XNs[:, t, :], X[:, X0 + t, :], mom[:, bass.ds(n0 + t, 1), 0],
                                                   rstd[:, bass.ds(n0 + t, 1)], ALU.subtract, ALU.mult)
                last.then_inc(xns_ready, 1)

            def lo(dst, src, h):
                return nc.vector.tensor_tensor(dst, src, h.bitcast(F32), ALU.subtract)

            nc.vector.memset(AOf[:, :], 1.0).then_inc(one_done, 1)
            nc.vector.memset(OTn[:, :, :], 0.0).then_inc(zero_done, 1)
            nc.vector.memset(decay[:, :], DECAY)
            dve.wait_ge(x_in[0], DMA)
            statistics(0, 0, TT, 1)
            for i in range(3):
                dve.wait_ge(whi_done, i + 1)
                raw = xf[:, 0, :] if i == 2 else qf[:, i, :]
                lo(WAl[:, i, :, :].rearrange("p k n -> p (k n)"), raw, WAh[:, i, :, :].rearrange("p k n -> p (k n)"))\
                    .then_inc(wlo_done, 1)
            dve.wait_ge(rstd_done, 1)
            normalise(0, 0, 0, True)
            for dt in range(KD):
                dve.wait_ge(x_hi, dt + 1)
                lo(xTl[:, 0, dt, :], xf[:, dt, :], xTh[:, 0, dt, :]).then_inc(x_lo, 1)
            for n in range(4):
                dve.wait_ge(qk_hi, n + 1)
                lo(ql[:, n % 2, :], qf[:, n % 2, :], qh[:, n % 2, :]).then_inc(qk_lo, 1)
            dve.wait_ge(whi_done, 4)
            lo(WOl[:, :, :].rearrange("p g n -> p (g n)"), vst[:, :, :].rearrange("p t n -> p (t n)"),
               WOh[:, :, :].rearrange("p g n -> p (g n)")).then_inc(wlo_done, 1)
            dve.wait_ge(had_copied, 1)
            for st in range(3):
                r = 1 << st
                src, dst = (PR[:, 4 * h:4 * h + 4, :].rearrange("p a n -> p (a n)")
                            .rearrange("p (m u r) -> p m u r", u=2, r=r * D) for h in (st % 2, 1 - st % 2))
                if st:
                    dve.wait_ge(fly_done, st)
                nc.vector.tensor_tensor(dst[:, :, 0, :], src[:, :, 0, :], src[:, :, 1, :], ALU.add)
                nc.vector.tensor_tensor(dst[:, :, 1, :], src[:, :, 0, :], src[:, :, 1, :], ALU.subtract).then_inc(fly_done, 1)
            for b in range(1, BATCH):
                dve.wait_ge(x_in[b], DMA)
            statistics(TT, TT, (BATCH - 1) * TT, 2)

            def row_max(b, kk):
                g, i = kk // 16, kk % 16
                dve.wait_ge(s1_ready, 32 * b + kk // 2 + 1)
                pair = kk // 2 % 2
                nc.vector.tensor_reduce(mxr[:, i - 1:i + 1], PS[:, 2 + 2 * pair:4 + 2 * pair, :], AX.X, ALU.max)\
                    .then_inc(max_done, 1)
                if i == 15:
                    s = 4 * b + g
                    dve.wait_ge(max_done, 8 * s + 8)
                    nc.vector.tensor_scalar(ms[:, 0, :].bitcast(F32R), mxr[:, :], -1.0, None, ALU.mult).then_inc(mh_done, 1)
                    dve.wait_ge(mh_done, s + 1)
                    nc.vector.scalar_tensor_tensor(ms[:, 1, :], mxr[:, :], -1.0, ms[:, 0, :], ALU.mult, ALU.subtract)\
                        .then_inc(ml_done, 1)
                    dve.wait_ge(ml_done, s + 1)

            def transpose_max(s, first=False):
                if not first:
                    dve.wait_ge(mscr_out, DMA * s)
                nc.vector.transpose(mT[:, :], ms[:, :, :].rearrange("p a k -> p (a k)")).then_inc(mt_ready, 1)

            for kk in range(1, AHEAD, 2):
                row_max(0, kk)
                if kk == 15:
                    transpose_max(0, True)

            def outputs(s, first=False):
                dve.wait_ge(av_done, 4 * s)
                nc.vector.transpose(OT[:, :, :].rearrange("p a c -> p (a c)"), OB).then_inc(ot_done, 1)
                dve.wait_ge(ot_done, s)
                nc.vector.reciprocal(rec[:, :], OT[:, :, HD]).then_inc(rec_done, 1)
                dve.wait_ge(rec_done, s)
                nc.vector.tensor_tensor(OTn[:, :, 0:HD], OT[:, :, 0:HD],
                                        rec[:, :].unsqueeze(2).broadcast_to([P, SEQ // 32, HD]), ALU.mult)\
                    .then_inc(otn_done, 1)
                dve.wait_ge(otn_done, s)
                dve.wait_ge(aol_done, s)
                nc.vector.transpose(AOf[:, :], OTn[:, :, :].rearrange("p a c -> p (a c)")).then_inc(aof_ready, 1)

            def add_attention(b, half, bank=MB):
                dve.wait_ge(wo_ready, 2 * b + half + 1)
                dve.wait_ge(bo_added, b + 1)
                v = X[:, bass.ds(TT * b + 2 * half, 2), :].rearrange("p t n -> p (t n)")
                nc.vector.tensor_tensor(v, v, bank, ALU.add).then_inc(x_done, 1)

            def slot(b, k, first, last):
                g, i = k // 16, k % 16
                kk = k + AHEAD
                if k in OUT_ADD and not first:
                    add_attention(b - 1, OUT_ADD.index(k))
                if k % 2:
                    if kk < SLOTS:
                        row_max(b, kk)
                        if kk % 16 == 15:
                            transpose_max(4 * b + kk // 16)
                    elif not last:
                        row_max(b + 1, kk - SLOTS)
                        if kk % 16 == 15:
                            transpose_max(4 * b + kk // 16)
                if i == 4 and not (first and g == 0):
                    outputs(4 * b + g)
                if k == 18:
                    if last:
                        dve.wait_ge(x_done, 2 * b)
                        statistics(0, 0, TT, 3)
                    else:
                        normalise(TT * (b + 1), TT * (b + 1), b + 1)
                if k == 23 and last:
                    dve.wait_ge(rstd_done, 3)
                    normalise(0, 0, BATCH)

            def tail(b):
                outputs(4 * b)
                for half in range(2):
                    add_attention(b - 1, half, PS[:, (7, 5)[half], :])

            dve.wait_ge(rstd_done, 2)
            windows(dve, slot, tail)

            def prepare(n, X0):
                statistics(X0, 0, TT, n + 4)

            def ffn_chunk(n, f0, c4, X0, last, split_mem=False):
                for f in range(FT):
                    dve.wait_ge(u_ready, FT * f0 + f + 1)
                    dve.wait_ge(sg_done, FT * f0 + f + 1)
                    nc.vector.tensor_tensor(PR[:, 2 + f % 2, :], PR[:, f % 2, :], PS[:, 2 + f % 2, :], ALU.mult)\
                        .then_inc(hf_done, 1)
                    dve.wait_ge(hh_done, FT * f0 + f + 1)
                    lo(AOl[:, f % 2, :], PR[:, 2 + f % 2, :], AOh[:, f % 2, :]).then_inc(hl_done, 1)
                    if f == 1 and not last:
                        dve.wait_ge(x_done, 2 * (n + BATCH))
                        pause()
                        prepare(n, X0)
                    if f == 3 and not last:
                        dve.wait_ge(rstd_done, n + 4)
                        normalise(X0, 0, n + BATCH + 1)
                    if split_mem and f == 5:
                        dve.wait_ge(w_in[W_MEM], DMA)
                        h, raw = (v[:, bass.ds(n * SEQ, SEQ)] for v in parts(W_MEM))
                        nc.vector.tensor_copy(h, raw.bitcast(F32)).then_inc(mem_hi, 1)
                    if split_mem and f == 6:
                        dve.wait_ge(mem_hi, n + 1)
                        lo(raw, raw.bitcast(F32), h).then_inc(mem_lo, 1)
                add_output(n, c4, 4)

            def add_output(n, c4, bank):
                for half in range(2):
                    dve.wait_ge(y_ready, 2 * n + half + 1)
                    v = X[:, bass.ds(c4 + 2 * half, 2), :].rearrange("p t n -> p (t n)")
                    nc.vector.tensor_tensor(v, v, PS[:, bank + half, :], ALU.add).then_inc(x_done, 1)

            def mem_chunk(n, c4, X0):
                c0 = n - BATCH
                dve.wait_ge(x_done, 2 * (n + BATCH))
                pause()
                prepare(n, X0)
                for m in range(KD):
                    dve.wait_ge(bsg_done, KD * c0 + m + 1)
                    dve.wait_ge(bv_ready, KD * c0 + m + 1)
                    store, mem = PR[:, 4 + m, :], PR[:, 6 + m, :]
                    nc.vector.scalar_tensor_tensor(store, PS[:, 3 * m, :], MSCALE, PR[:, m, :], ALU.mult, ALU.mult)\
                        .then_inc(bst2_done, 1)
                    dve.wait_ge(bst2_done, KD * c0 + m + 1)
                    nc.vector.tensor_tensor_scan(mem, decay[:, 0:1].broadcast_to([P, SEQ]), store, 0.0, ALU.mult, ALU.add)\
                        .then_inc(scan_done, 1)
                    dve.wait_ge(scan_done, KD * c0 + m + 1)
                    dve.wait_ge(bsq_done, KD * c0 + m + 1)
                    nc.vector.scalar_tensor_tensor(store, mem, MSCALE, PR[:, 2 + m, :], ALU.mult, ALU.mult)\
                        .then_inc(load_done, 1)
                    if m == 0:
                        dve.wait_ge(rstd_done, n + 4)
                        normalise(X0, 0, n + BATCH + 1)
                    dve.wait_ge(lh_done, KD * c0 + m + 1)
                    lo(AOl[:, m, :], store, AOh[:, m, :]).then_inc(ll_done, 1)
                add_output(n, c4, 6)

            def following(i, cc):
                return TT * (2 * i + 1) if cc == 0 else 2 * TT * (1 - i)

            with dve.Fori(0, 2) as i:
                for cc in range(2):
                    ffn_chunk(2 * i + cc, 2 * i + cc, TT * (2 * i + cc), following(i, cc), False, True)
            with dve.Fori(0, 2) as i:
                for cc in range(2):
                    mem_chunk(BATCH + 2 * i + cc, TT * (2 * i + cc), following(i, cc))
            for c in range(BATCH):
                ffn_chunk(2 * BATCH + c, BATCH + c, TT * c, TT * ((c + 1) % BATCH), c == BATCH - 1)

        @block.gpsimd
        def _(pool):
            def reciprocal_deviation(n0, count, n):
                pool.wait_ge(mom_done, n)
                nc.gpsimd.tensor_tensor(veps[:, n0:n0 + count], mom[:, n0:n0 + count, 1], eps[:, n0:n0 + count], ALU.add)\
                    .then_inc(veps_done, 1)
                pool.wait_ge(veps_done, n)
                nc.gpsimd.tensor_tensor(rstd[:, n0:n0 + count], veps[:, n0:n0 + count], mhalf[:, n0:n0 + count], ALU.pow)\
                    .then_inc(rstd_done, 1)

            def lo(dst, src, h):
                return nc.gpsimd.tensor_tensor(dst, src, h.bitcast(F32), ALU.subtract)

            def x_lo_part(L, dt, par):
                pool.wait_ge(x_hi, 2 * L + dt + 1)
                lo(xTl[:, par, dt, :], xf[:, dt, :], xTh[:, par, dt, :]).then_inc(x_lo, 1)

            def qk_lo_part(b, n):
                pool.wait_ge(qk_hi, 4 * b + n + 1)
                lo(ql[:, n % 2, :], qf[:, n % 2, :], qh[:, n % 2, :]).then_inc(qk_lo, 1)

            def place_values(b, g, fresh=False):
                pool.wait_ge(v_copied, 2 * b + 2)
                if not fresh:
                    pool.wait_ge(av_done, 16 * b + 4 * g - 12)
                cs = slice(g * GH * HD, (g + 1) * GH * HD)
                nc.gpsimd.tensor_tensor(Vp[:, :, GH * g:GH * (g + 1), 0:HD],
                                        vst[:, :, cs].rearrange("p t (h c) -> p t h c", c=HD),
                                        bvt[:, cs].rearrange("p (h c) -> p h c", c=HD).unsqueeze(1)
                                        .broadcast_to([P, TT, GH, HD]), ALU.add).then_inc(vp_ready, 1)

            def output_lo(s, g):
                pool.wait_ge(aoh_done, s)
                lo(AOl[:, g, :], AOf[:, :], AOh[:, g, :]).then_inc(aol_done, 1)

            def add_bo(b):
                v = X[:, bass.ds(TT * b, TT), :]
                nc.gpsimd.tensor_tensor(v, v, bot[:, :].unsqueeze(1).broadcast_to([P, TT, D]), ALU.add).then_inc(bo_added, 1)

            nc.gpsimd.memset(mhalf[:, :], -0.5)
            nc.gpsimd.memset(eps[:, :], EPS).then_inc(pool_init, 1)
            nc.gpsimd.memset(Vp[:, :, :, HD:HD + 1], 1.0).then_inc(pool_init, 1)
            nc.gpsimd.memset(Vp[:, :, :, HD + 1:], 0.0).then_inc(hf_done, 2)
            pool.wait_ge(pool_init, 2)
            reciprocal_deviation(0, TT, 1)
            pool.wait_ge(const_in, 3 * DMA)
            for g in range(GROUPS):
                place_values(0, g, True)
            pool.wait_ge(xns_ready, 1)
            reciprocal_deviation(TT, (BATCH - 1) * TT, 2)
            add_bo(0)

            def slot(b, k, first, last):
                if k == 7 and not first:
                    output_lo(4 * b, GROUPS - 1)
                if k == 9 and not first:
                    place_values(b, GROUPS - 1)
                if k == 18 and not last:
                    pool.wait_ge(xns_ready, b + 2)
                    add_bo(b + 1)
                if k == 18 and last:
                    reciprocal_deviation(0, TT, 3)
                for dt in range(KD):
                    if k == LN_PE[dt] + 6 * last + 1:
                        x_lo_part(b + 1, dt, 0)
                if k in (24, 40, 56):
                    output_lo(4 * b + k // 16, k // 16 - 1)
                if not last:
                    if k - 3 in QK_PE:
                        qk_lo_part(b + 1, QK_PE.index(k - 3))
                    if k in V_PLACE:
                        place_values(b + 1, V_PLACE.index(k))
                elif k in SPLIT_AT:
                    n = SPLIT_AT.index(k)
                    pool.wait_ge(lhi_done, n + 1)
                    h, raw = quarter(n // 4, n % 4)
                    lo(raw, raw.bitcast(F32), h).then_inc(llo_done, 1)

            nc.gpsimd.memset(credit[:, :], 0.0).then_inc(aol_done, 1)
            windows(pool, slot, lambda b: output_lo(4 * b, GROUPS - 1))

            def prepare(n, par):
                reciprocal_deviation(0, TT, n + 4)
                for dt in range(KD):
                    x_lo_part(n + BATCH + 1, dt, 1 - par)

            for n0 in (0, BATCH):
                with pool.Fori(0, 2) as i:
                    for cc in range(2):
                        prepare(n0 + 2 * i + cc, cc)
            for c in range(BATCH - 1):
                prepare(2 * BATCH + c, c % 2)


def kernel(**inputs):
    import numpy as np
    import concourse.bacc as bacc
    from concourse import mybir as mb
    from concourse.bass_utils import run_bass_kernel_spmd as run

    a = {k.split("_", 1)[1]: np.asarray(v) for k, v in inputs.items()}
    order = np.arange(D).reshape(2, HEADS // 2, HD).transpose(0, 2, 1).reshape(-1)
    wo = np.zeros((GROUPS, GH, 32, D), np.float32)
    wo[:, :, :HD, :] = a["attn_a_Wo"].T.reshape(GROUPS, GH, HD, D)
    bqk = np.stack([a["attn_a_bq"][order].reshape(KD, P), a["attn_a_bk"][order].reshape(KD, P)], 1).reshape(2 * KD, P).T
    bgq = np.concatenate([a["attn_b_bg"].reshape(KD, P), a["attn_b_bq"].reshape(KD, P)]).T
    had = np.ones((1, 1), np.float32)
    while had.shape[0] < P:
        had = np.block([[had, had], [had, -had]])
    arrays = {
        "x": a["attn_a_x"], "wq": a["attn_a_Wq"].T[:, order], "wk": a["attn_a_Wk"].T[:, order],
        "wv": a["attn_a_Wv"].T, "wo": wo.reshape(GROUPS, P, D), "bqk_d": bqk, "bgq_d": bgq, "bv": a["attn_a_bv"], "bo": a["attn_a_bo"],
        "mv_": a["attn_b_Wv"], "mg": a["attn_b_Wg"], "mq": a["attn_b_Wq"], "mo": a["attn_b_Wo"], "w1": a["ffn_W1"].T, "w2": a["ffn_W2"].T,
        "w3": a["ffn_W3"].T, "ident_d": np.eye(P, dtype=np.float32), "had_d": had.astype(np.float32),
    }
    arrays = {k: np.ascontiguousarray(v) for k, v in arrays.items()}
    nc = bacc.Bacc("TRN2", target_bir_lowering=False, num_devices=1)
    args = {k: nc.dram_tensor(f"in_{k}", v.shape, mb.dt.from_np(v.dtype), kind="ExternalInput").ap()
            for k, v in arrays.items()}
    args["out"] = nc.dram_tensor("out_0", [BATCH, SEQ, D], F32, kind="ExternalOutput").ap()
    build(nc, **args)
    got = run(nc, [{f"in_{k}": v for k, v in arrays.items()}], core_ids=[0])
    return got.results[0]["out_0"]
```

```python
from contextlib import ExitStack

import concourse.bass as bass
from concourse import mybir

F32 = mybir.dt.float32
F32R = mybir.dt.float32r
ALU = mybir.AluOpType
ACT = mybir.ActivationFunctionType
AX = mybir.AxisListType

P = 128
BATCH, SEQ, D = 4, 512, 256
HEADS, HD = 16, 16
HID = 1024
TT = SEQ // P
KD = D // P
GROUPS = 4
GH = HEADS // GROUPS
FT = HID // P
SLOTS = GROUPS * TT * GH
AHEAD = 25
TURN = 14
OUT_PE, OUT_ADD = (5, 9), (9, 13)
LN_PE = (18, 20)
STAT_AT, NORM_AT = (40, 41, 42, 43), (53, 54, 55, 56)
LN_LATER = 42
QK_PE, QK_OUT = (21, 25, 29, 33), (25, 29, 33, 37)
RING_IN = (26, 30, 34, 49)
V_PE, V_PLACE = (38, 42), (48, 49, 57)
QUIET = (SLOTS - AHEAD + 3) // 4 * 4
SPLIT_AT = (41, 42, 43, 44, 45, 46, 47, 54, 57, 59, 61, 63)
OUT_SLOT = 2
LAG = 2
QROWS = 4 * HD
MROW = 96
DMA = 16
EPS = 1e-5
DECAY = 0.95
MSCALE = float((1.0 - DECAY) ** 0.5)
QI, KI = 0, 1


def build(nc, x, wq, wk, wv, wo, bqk_d, bv, bo, mv_, mg, mq, bgq_d, mo, w1, w2, w3, ident_d, had_d, out):
    ctx = ExitStack()
    with ctx:
        def sb(name, shape, dt=F32):
            return ctx.enter_context(nc.sbuf_tensor(name, shape, dt))

        def sem(name):
            return ctx.enter_context(nc.semaphore(name))

        X = sb("X", [P, BATCH * TT, D])
        XNs = sb("XNs", [P, TT, D])
        xf = sb("xf", [P, KD, SEQ])
        xTh = sb("xTh", [P, 2, KD, SEQ], F32R)
        xTl = sb("xTl", [P, 2, KD, SEQ], F32R)
        ring = sb("ring", [P, GROUPS, 2, GH, SEQ], F32R)
        PR = sb("PR", [P, 8, SEQ])
        Vp = sb("Vp", [P, TT, HEADS, 2 * HD])
        vst = sb("vst", [P, TT, D])
        qf = sb("qf", [P, 2, SEQ])
        qh = sb("qh", [P, 2, SEQ], F32R)
        ql = sb("ql", [P, 2, SEQ], F32R)
        OT = sb("OT", [P, SEQ // 32, 32])
        OTn = sb("OTn", [P, SEQ // 32, 32])
        AOf = sb("AOf", [P, SEQ])
        AOh = sb("AOh", [P, GROUPS, SEQ], F32R)
        AOl = sb("AOl", [P, GROUPS, SEQ], F32R)
        WAh = sb("WAh", [P, 3, KD, D], F32R)
        WAl = sb("WAl", [P, 3, KD, D], F32R)
        WOh = sb("WOh", [P, GROUPS, D], F32R)
        WOl = sb("WOl", [P, GROUPS, D], F32R)
        bqk = sb("bqk", [P, 4])
        bgq = sb("bgq", [P, 4])
        bvt = sb("bvt", [P, D])
        bot = sb("bot", [P, D])
        ident = sb("ident", [P, P])
        had = sb("had", [P, P])
        mxr = sb("mxr", [P, 2, GH * TT])
        ms = sb("ms", [P, 2, GH * TT])
        mT = sb("mT", [P, 32])
        rec = sb("rec", [P, SEQ // 32])
        bst = sb("bst", [P, BATCH * TT, 6])
        mom = sb("mom", [P, BATCH * TT, 2])
        veps = sb("veps", [P, BATCH * TT])
        rstd = sb("rstd", [P, BATCH * TT])
        eps = sb("eps", [P, BATCH * TT])
        mhalf = sb("mhalf", [P, BATCH * TT])
        decay = sb("decay", [P, 1])
        spare = sb("spare", [P, 1])
        credit = sb("credit", [P, 1])
        PS = ctx.enter_context(nc.psum_tensor("PS", [P, 8, SEQ], F32))
        OB, MB = PS[:, 6, :], PS[:, 7, :]
        qscr = nc.dram_tensor("qk_scratch", [BATCH, 2, 2, 2, HD, HEADS // 2, SEQ], F32, kind="Internal").ap()
        mscr = nc.dram_tensor("max_scratch", [GROUPS, 2 * GH * TT, P // 32, 32], F32, kind="Internal").ap()
        wscr = nc.dram_tensor("weight_scratch", [4, P, KD * HID], F32, kind="Internal").ap()
        W_UP, W_LIN, W_DOWN, W_MEM = range(4)

        def parts(slot):
            v = ring[:, slot, :, :, :].rearrange("p a h n -> p a (h n)")
            return v[:, 0, :], v[:, 1, :]

        def quarter(slot, i):
            return tuple(v[:, i * SEQ:(i + 1) * SEQ] for v in parts(slot))

        x_in = [sem(f"x_in{b}") for b in range(BATCH)]
        wqk_in, wv_in, wo_in, bias_in, ident_in, const_in = (sem(n) for n in ("wqk_in", "wv_in", "wo_in", "bias_in",
                                                                          "ident_in", "const_in"))
        w2_in = sem("w2_in")
        fill_in = [sem(f"fill_in{g}") for g in range(GROUPS)]
        wol_done = sem("wol_done")
        zero_done, one_done, pool_init, whi_done, wlo_done, had_ready, had_copied, fly_done = (
            sem(n) for n in ("zero_done", "one_done", "pool_init", "whi_done", "wlo_done", "had_ready",
                             "had_copied", "fly_done"))
        bst_done, mom_done, veps_done, rstd_done, xns_ready, lnT_ready, x_f, x_hi, x_lo = (
            sem(n) for n in ("bst_done", "mom_done", "veps_done", "rstd_done", "xns_ready", "lnT_ready", "x_f", "x_hi",
                             "x_lo"))
        qk_ready, qk_f, qk_hi, qk_lo, v_ready, v_copied, vp_ready, bo_added = (
            sem(n) for n in ("qk_ready", "qk_f", "qk_hi", "qk_lo", "v_ready", "v_copied", "vp_ready", "bo_added"))
        scr_out = [sem("scr_out0"), sem("scr_out1")]
        ring_in = [sem(f"ring_in{g}") for g in range(GROUPS)]
        s1_ready, max_done, mh_done, ml_done, mt_ready, mscr_out = (
            sem(n) for n in ("s1_ready", "max_done", "mh_done", "ml_done", "mt_ready", "mscr_out"))
        mrow_in = [sem(f"mrow_in{g}") for g in range(GROUPS)]
        st_ready, exp_done, av_done, ot_done, rec_done, otn_done, aof_ready, aoh_done, aol_done, wo_ready, x_done = (
            sem(n) for n in ("st_ready", "exp_done", "av_done", "ot_done", "rec_done", "otn_done", "aof_ready",
                             "aoh_done", "aol_done", "wo_ready", "x_done"))
        scr_w = [sem(f"scr_w{g}") for g in range(4)]
        w_in = [sem(f"w_in{g}") for g in range(4)]
        lhi_done, llo_done, mem_hi, mem_lo = (sem(n) for n in ("lhi_done", "llo_done", "mem_hi", "mem_lo"))
        g_ready, u_ready, sg_done, hf_done, hh_done, hl_done, y_ready = (
            sem(n) for n in ("g_ready", "u_ready", "sg_done", "hf_done", "hh_done", "hl_done", "y_ready"))
        bg_ready, bq_ready, bv_ready, bsg_done, bsq_done, bst2_done, scan_done, load_done, lh_done, ll_done = (
            sem(n) for n in ("bg_ready", "bq_ready", "bv_ready", "bsg_done", "bsq_done", "bst2_done", "scan_done",
                             "load_done", "lh_done", "ll_done"))
        out_done = sem("out_done")

        def windows(eng, slot, tail):
            for k in range(TURN):
                slot(0, k, True, False)
            with eng.Fori(0, BATCH - 1) as b:
                for k in range(TURN, SLOTS):
                    slot(b, k, False, False)
                for k in range(TURN):
                    slot(b + 1, k, False, False)
            for k in range(TURN, SLOTS):
                slot(BATCH - 1, k, False, True)
            tail(BATCH)

        block = ctx.enter_context(nc.Block())

        @block.sync
        def _(sp):
            xv = x.rearrange("b (t p) d -> b p t d", p=P)
            sp.dma_start(X[:, 0:TT, :], xv[0, :, :, :]).then_inc(x_in[0], DMA)
            for i, w in enumerate((wq, wk)):
                sp.dma_start(qf[:, i, :].rearrange("p (k n) -> p k n", k=KD),
                             w.rearrange("(k p) n -> p k n", p=P)).then_inc(wqk_in, DMA)
            sp.dma_start(xf[:, 0, :].rearrange("p (k n) -> p k n", k=KD),
                         wv.rearrange("(k p) n -> p k n", p=P)).then_inc(wv_in, DMA)
            sp.dma_start(ident[:, :], ident_d).then_inc(ident_in, DMA)
            sp.dma_start(bqk[:, :], bqk_d).then_inc(bias_in, DMA)
            sp.dma_start(PR[:, 0:4, :].rearrange("p a (u n) -> p (a u) n", n=D),
                         w2.rearrange("(f p) n -> p f n", p=P)).then_inc(w2_in, DMA)
            sp.dma_start(had[:, :], had_d).then_inc(w2_in, DMA)
            sp.dma_start(vst[:, :, :], wo.rearrange("g p n -> p g n")).then_inc(wo_in, DMA)

            def constant_rows(g):
                sp.dma_start(ring[QROWS:MROW, g, :, :, :].rearrange("p a h n -> p (a h) n").bitcast(F32),
                             OTn[0:MROW - QROWS, :, :].rearrange("p a c -> p (a c)").unsqueeze(1)
                             .broadcast_to([MROW - QROWS, 2 * GH, SEQ])).then_inc(fill_in[g], DMA)
                sp.dma_start(ring[MROW:MROW + 2, g, KI, :, :].bitcast(F32),
                             AOf[0:2, :].unsqueeze(1).broadcast_to([2, GH, SEQ])).then_inc(fill_in[g], DMA)

            sp.wait_ge(zero_done, 1)
            sp.wait_ge(one_done, 1)
            constant_rows(0)
            for b in range(1, BATCH):
                sp.dma_start(X[:, b * TT:(b + 1) * TT, :], xv[b, :, :, :]).then_inc(x_in[b], DMA)
            sp.dma_start(bvt[:, :], bv.partition_broadcast(P)).then_inc(const_in, DMA)
            sp.dma_start(bot[:, :], bo.partition_broadcast(P)).then_inc(const_in, DMA)
            sp.dma_start(bgq[:, :], bgq_d).then_inc(const_in, DMA)

            def scratch_out(b, n):
                sp.wait_ge(qk_lo, 4 * b + n + 1)
                mt, qk = n // 2, n % 2
                for part, t in ((0, qh), (1, ql)):
                    sp.dma_start(qscr[b, qk, part, mt, :, :, :].rearrange("r h n -> (r h) n"),
                                 t[:, n % 2, :].bitcast(F32)).then_inc(scr_out[n % 2], DMA)

            def ring_load(b, g, only=None):
                mt, h0 = g // 2, GH * (g % 2)
                for qk in (QI, KI) if only is None else (only,):
                    sp.wait_ge(scr_out[qk], 2 * DMA * (2 * b + mt + 1))
                    for a in range(2):
                        dst = ring[32 * a:32 * a + 32, g, qk, :, :].rearrange("p h n -> p (h n)").bitcast(F32)
                        if qk == QI:
                            src = qscr[b, qk, a, mt, :, h0:h0 + GH, :].rearrange("r h n -> r (h n)")
                            src = src.unsqueeze(0).broadcast_to([2, HD, GH * SEQ])
                        else:
                            src = qscr[b, qk, :, mt, :, h0:h0 + GH, :].rearrange("a r h n -> a r (h n)")
                        sp.dma_start(dst, src).then_inc(ring_in[g], DMA)

            def max_rows(b, g):
                sp.wait_ge(mt_ready, 4 * b + g + 1)
                sp.dma_start(mscr[g, :, :, :].rearrange("k c n -> c k n"), mT[:, :]).then_inc(mscr_out, DMA)
                sp.wait_ge(mscr_out, DMA * (4 * b + g + 1))
                sp.dma_start(ring[MROW:MROW + 2, g, QI, :, :].rearrange("p h n -> p (h n)").bitcast(F32),
                             mscr[g, :, :, :].rearrange("(a k) c n -> a (k c n)", a=2)).then_inc(mrow_in[g], DMA)

            def weights_in(w):
                sp.wait_ge(st_ready, SLOTS * (BATCH - 1) + 16 * (w + 1))
                sp.wait_ge(scr_w[w], (4 if w == W_MEM else 1) * DMA)
                sp.dma_start(parts(w)[1].bitcast(F32), wscr[w, :, :]).then_inc(w_in[w], DMA)

            def layout(w, j, k, src):
                sp.dma_start(wscr[w, :, j * SEQ:(j + k) * SEQ].rearrange("p (k n) -> p k n", k=KD),
                             src.rearrange("(k p) n -> p k n", p=P)).then_inc(scr_w[w], DMA)

            scratch_out(0, 0)
            scratch_out(0, 1)
            ring_load(0, 0)
            constant_rows(1)
            ring_load(0, 1)
            for n in range(2, 4):
                scratch_out(0, n)
            constant_rows(2)
            ring_load(0, 2)
            max_rows(0, 0)
            sp.wait_ge(fly_done, 3)
            sp.dma_start(wscr[W_DOWN, :, :], PR[:, 4:8, :].rearrange("p a n -> p (a n)")).then_inc(scr_w[W_DOWN], DMA)
            constant_rows(3)
            ring_load(0, 3)

            def slot(b, k, first, last):
                g, i = k // 16, k % 16
                if k == 1 and not first:
                    sp.wait_ge(st_ready, SLOTS * b)
                    ring_load(b, 3)
                if i == 9 and not (last and g == 3):
                    max_rows(b + (g + 1) // GROUPS, (g + 1) % GROUPS)
                if first and k == 10:
                    layout(W_UP, 0, 4, w1)
                    layout(W_LIN, 0, 4, w3)
                if first and k == TURN - 1:
                    for j, src in enumerate((mv_, mg, mq, mo)):
                        layout(W_MEM, j, 1, src)
                if not last:
                    if k in QK_OUT:
                        scratch_out(b + 1, QK_OUT.index(k))
                    if k in RING_IN:
                        g1, qk = ((0, QI), (0, KI), (1, None), (2, None))[RING_IN.index(k)]
                        sp.wait_ge(st_ready, SLOTS * b + 16 * (g1 + 1))
                        ring_load(b + 1, g1, qk)
                elif k in (19, 33, 49):
                    weights_in(g - 1)

            windows(sp, slot, lambda b: weights_in(W_MEM))
            ov = out.rearrange("b (t p) d -> b p t d", p=P)
            for c in range(BATCH):
                sp.wait_ge(x_done, 2 * (BATCH + 2 * BATCH + c + 1))
                sp.dma_start(ov[c, :, :, :], X[:, c * TT:(c + 1) * TT, :]).then_inc(out_done, DMA)
            sp.wait_ge(out_done, DMA * BATCH)

        @block.tensor
        def _(pe):
            def mm(dst, lhsT, rhs, start, stop):
                return nc.tensor.matmul(dst, lhsT, rhs, start=start, stop=stop, skip_group_check=True)

            def split_mm(dst, pairs, start=True, stop=True):
                n = 3 * len(pairs)
                ops = [(l, r) for ll, lh, rl, rh in pairs for l, r in ((ll, rh), (lh, rl), (lh, rh))]
                for i, (l, r) in enumerate(ops):
                    last = mm(dst, l, r, start and i == 0, stop and i == n - 1)
                return last

            def ln_transpose(L, dt, bank):
                for t in range(TT):
                    last = nc.tensor.transpose(bank[:, t * P:(t + 1) * P], XNs[:, t, dt * P:(dt + 1) * P], ident[:, :])
                last.then_inc(lnT_ready, 1)

            def xt(par, kt):
                return xTl[:, par, kt, :], xTh[:, par, kt, :]

            def project_qk(b, n, part, bank=MB):
                w, m = n % 2, n // 2 * P
                ops = [(1, 1, 0), (1, 1, 1), (0, 1, 0), (0, 1, 1), (0, 0, 0), (0, 0, 1)]
                if n == 0 and part == 2:
                    pe.wait_ge(x_lo, 2 * (b + 1))
                for i in (2 * part, 2 * part + 1):
                    lo, r, kt = ops[i]
                    lhsT = (WAl if lo else WAh)[:, w, kt, m:m + P]
                    last = mm(bank, lhsT, xt(0, kt)[r], i == 0, i == 5)
                if part == 2:
                    last.then_inc(qk_ready, 1)

            def project_v(b, half, part, bank=MB):
                ops = [(t, kt, l, w) for t in range(2) for kt in range(KD) for l, w in ((0, WAh), (1, WAl), (1, WAh))]
                for i in range(4 * part, 4 * part + 4):
                    t, kt, l, w = ops[i]
                    tok = (2 * half + t) * P
                    last = mm(bank[:, t * D:(t + 1) * D], xt(0, kt)[l][:, tok:tok + P], w[:, 2, kt, :],
                              i % 6 == 0, i % 6 == 5)
                if part == 2:
                    last.then_inc(v_ready, 1)

            def out_projection(b, half, part):
                for t in range(2):
                    ts = slice((2 * half + t) * P, (2 * half + t + 1) * P)
                    last = split_mm(MB[:, t * D:(t + 1) * D],
                                    [(AOl[:, part, ts], AOh[:, part, ts], WOl[:, part, :], WOh[:, part, :])],
                                    part == 0 and t == 0, part == GROUPS - 1)
                if part == 3:
                    last.then_inc(wo_ready, 1)

            def score_qk(b, kk, fresh=False, first=False):
                g, i = kk // 16, kk % 16
                j, t = i // TT, i % TT
                if i == 0:
                    pe.wait_ge(ring_in[g], 4 * DMA * (b + 1))
                    if fresh or first:
                        pe.wait_ge(fill_in[g], 2 * DMA)
                if not (fresh and kk < 3):
                    pe.wait_ge(max_done, SLOTS * b + (kk and kk - 2))
                mm(PS[:, 3 + kk % 3, :], ring[0:MROW, g, QI, j, t * P:(t + 1) * P], ring[0:MROW, g, KI, j, :],
                   True, True).then_inc(s1_ready, 1)

            def score_kq(b, k, first):
                g, i = k // 16, k % 16
                if first and k == 0:
                    pe.wait_ge(v_copied, 2)
                kt, j = i // GH, i % GH
                if i == 0:
                    pe.wait_ge(mrow_in[g], DMA * (b + 1))
                if not (first and k < 3):
                    pe.wait_ge(exp_done, SLOTS * b + (k and k - 2))
                mm(PS[:, k % 3, :], ring[0:MROW + 2, g, KI, j, kt * P:(kt + 1) * P], ring[0:MROW + 2, g, QI, j, :],
                   True, True).then_inc(st_ready, 1)

            def weigh_values(b, g, kt, first=False):
                s = 4 * b + g
                pe.wait_ge(exp_done, 16 * s + 4 * kt + 4)
                if kt == 0:
                    pe.wait_ge(vp_ready, s + 1)
                    if not first:
                        pe.wait_ge(ot_done, s)
                for j in range(GH):
                    last = mm(OB[32 * j:32 * j + 32, :], Vp[:, kt, GH * g + j, :], PR[:, (4 * kt + j) % 8, :],
                              kt == 0, kt == TT - 1)
                last.then_inc(av_done, 1)

            pe.wait_ge(ident_in, DMA)
            pe.wait_ge(xns_ready, 1)
            for dt in range(KD):
                ln_transpose(0, dt, PS[:, dt, :])
            pe.wait_ge(wlo_done, 3)
            pe.wait_ge(x_hi, 2)
            for n in range(4):
                if n == 2:
                    pe.wait_ge(w2_in, 2 * DMA)
                    pe.wait_ge(x_f, 2)
                    for j in range(FT // 2):
                        last = mm(PS[:, (0, 1, 6, 7)[j], :], had[:, :], PR[:, j, :], True, True)
                    last.then_inc(had_ready, 1)
                for part in range(3):
                    project_qk(0, n, part, PS[:, 2 + n, :])
            pe.wait_ge(had_copied, 1)
            for half in range(2):
                for part in range(3):
                    project_v(0, half, part, PS[:, half, :])
            pe.wait_ge(qk_f, 4)
            pe.wait_ge(qk_hi, 4)
            for kk in range(AHEAD):
                score_qk(0, kk, True)

            def slot(b, k, first, last):
                g, i = k // 16, k % 16
                score_kq(b, k, first)
                if first and k == TURN - 1:
                    pe.wait_ge(fill_in[GROUPS - 1], 2 * DMA)
                if i % 4 == (2 if last and k >= QUIET else 1):
                    if i > 3:
                        weigh_values(b, g, i // 4 - 1, first and g == 0)
                    elif g:
                        weigh_values(b, g - 1, TT - 1, first and g == 1)
                    elif not first:
                        weigh_values(b - 1, GROUPS - 1, TT - 1)
                kk = k + AHEAD
                if kk < SLOTS:
                    score_qk(b, kk, False, first)
                elif not last:
                    score_qk(b + 1, kk - SLOTS)
                if not first and (OUT_PE[0] <= k < OUT_PE[0] + 4 or OUT_PE[1] <= k < OUT_PE[1] + 4):
                    if k == OUT_PE[0]:
                        pe.wait_ge(aol_done, 4 * b)
                        pe.wait_ge(v_copied, 2 * b + 2)
                    if k == OUT_PE[0] + 3:
                        pe.wait_ge(aol_done, 4 * b + 1)
                    half = int(k >= OUT_PE[1])
                    if k == OUT_PE[1]:
                        pe.wait_ge(x_done, 2 * b - 1)
                    out_projection(b - 1, half, k - OUT_PE[half])
                if k == LN_PE[0] + LN_LATER * last:
                    pe.wait_ge(xns_ready, b + 2)
                    ln_transpose(b + 1, 0, MB)
                if k == LN_PE[1] + LN_LATER * last:
                    pe.wait_ge(x_f, 2 * b + 3)
                    ln_transpose(b + 1, 1, MB)
                if not last:
                    for n, k0 in enumerate(QK_PE):
                        if k == k0 and n == 0:
                            pe.wait_ge(x_hi, 2 * b + 4)
                        elif k == k0:
                            pe.wait_ge(qk_f, 4 * b + 4 + n)
                        if k0 <= k < k0 + 3:
                            project_qk(b + 1, n, k - k0)
                    for half, k0 in enumerate(V_PE):
                        if k == k0 and half == 0:
                            pe.wait_ge(qk_f, 4 * b + 8)
                        elif k == k0:
                            pe.wait_ge(v_copied, 2 * b + 3)
                        if k0 <= k < k0 + 3:
                            project_v(b + 1, half, k - k0)

            def tail(b):
                weigh_values(b - 1, GROUPS - 1, TT - 1)
                pe.wait_ge(x_f, 2 * b + 2)
                pe.wait_ge(max_done, SLOTS * b)
                for g in range(GROUPS):
                    if g in (0, GROUPS - 1):
                        pe.wait_ge(aol_done, 4 * b + (g > 0))
                    for t in range(TT):
                        ts = slice(t * P, (t + 1) * P)
                        last = split_mm(PS[:, (7, 5)[t // 2], t % 2 * D:(t % 2 + 1) * D],
                                        [(AOl[:, g, ts], AOh[:, g, ts], WOl[:, g, :], WOh[:, g, :])],
                                        g == 0 and t % 2 == 0, g == GROUPS - 1)
                        if g == GROUPS - 1 and t % 2:
                            last.then_inc(wo_ready, 1)

            windows(pe, slot, tail)

            def ffn_chunk(n, f0, par, last, left=None):
                w1h, w1l = (v.rearrange("p (k n) -> p k n", k=KD) for v in parts(W_UP))
                w3h, w3l = (v.rearrange("p (k n) -> p k n", k=KD) for v in parts(W_LIN))
                w2h, w2l = (v.rearrange("p (f n) -> p f n", f=FT) for v in parts(W_DOWN))

                def down(f):
                    if f == 0:
                        pe.wait_ge(x_done, 2 * (n + BATCH))
                    pe.wait_ge(hl_done, FT * f0 + f + 1)
                    for t in range(TT):
                        ts = slice(t * P, (t + 1) * P)
                        last_ = split_mm(PS[:, 4 + t // 2, t % 2 * D:(t % 2 + 1) * D],
                                         [(AOl[:, f % 4, ts], AOh[:, f % 4, ts], w2l[:, f, :], w2h[:, f, :])],
                                         f == 0 and t % 2 == 0, f == FT - 1)
                        if f == FT - 1 and t % 2:
                            last_.then_inc(y_ready, 1)

                pe.wait_ge(x_lo, 2 * (n + BATCH + 1))
                for f in range(FT):
                    fs = slice(f * P, (f + 1) * P)
                    pe.wait_ge(hf_done, FT * f0 + f + 1)
                    for bank, wl, wh, ready in ((f % 2, w1l, w1h, g_ready), (2 + f % 2, w3l, w3h, u_ready)):
                        split_mm(PS[:, bank, :], [(wl[:, k, fs], wh[:, k, fs]) + xt(par, k) for k in range(KD)])\
                            .then_inc(ready, 1)
                    if left and f == 0:
                        left()
                    if f >= LAG:
                        down(f - LAG)
                    if f == 4 and not last:
                        pe.wait_ge(xns_ready, n + BATCH + 2)
                        ln_transpose(n + 1, 0, PS[:, 6, :])
                        ln_transpose(n + 1, 1, PS[:, 7, :])
                for f in range(FT - LAG, FT):
                    down(f)

            def memory_phase():
                wh, wl = (v.rearrange("p (w k n) -> p w k n", w=4, k=KD) for v in parts(W_MEM))
                tiles = ((1, bg_ready), (0, bv_ready), (2, bq_ready))

                def products(par, m, w, x_lo_part, x_hi_part, ready=None):
                    ms_ = slice(m * P, (m + 1) * P)
                    ops = [(wt[:, w, k, ms_], xTh[:, par, k, :]) for k in range(KD) for wt in (wl, wh)] * x_hi_part
                    ops += [(wh[:, w, k, ms_], xTl[:, par, k, :]) for k in range(KD)] * x_lo_part
                    for i, (l, r) in enumerate(ops):
                        last = mm(PS[:, 3 * m + w, :], l, r, i == 0 and x_hi_part, i == len(ops) - 1 and x_lo_part)
                    if ready:
                        last.then_inc(ready, 1)

                def load_out(c, m):
                    pe.wait_ge(ll_done, KD * c + m + 1)
                    for t in range(TT):
                        ts = slice(t * P, (t + 1) * P)
                        last = split_mm(PS[:, 6 + t // 2, t % 2 * D:(t % 2 + 1) * D],
                                        [(AOl[:, m, ts], AOh[:, m, ts], wl[:, 3, m, :], wh[:, 3, m, :])],
                                        m == 0 and t % 2 == 0, m == KD - 1)
                        if m == KD - 1 and t % 2:
                            last.then_inc(y_ready, 1)

                pe.wait_ge(x_lo, 2 * (2 * BATCH + 1))
                for w, ready in tiles:
                    products(0, 0, w, True, True, ready)
                pe.wait_ge(x_done, 4 * BATCH)
                for c in range(BATCH):
                    n = BATCH + c
                    for w, ready in tiles:
                        if w == 2:
                            pe.wait_ge(xns_ready, n + BATCH + 2)
                            for dt in range(KD):
                                ln_transpose(n + 1, dt, PS[:, 6 + dt, :])
                        products(c % 2, 1, w, True, True, ready)
                    pe.wait_ge(x_f, 2 * (n + BATCH + 2))
                    load_out(c, 0)
                    if c < BATCH - 1:
                        pe.wait_ge(x_hi, 2 * (n + BATCH + 2))
                        for w, _ in tiles:
                            products(1 - c % 2, 0, w, False, True)
                    if c < BATCH - 1:
                        load_out(c, 1)
                        pe.wait_ge(x_lo, 2 * (n + BATCH + 2))
                        for w, ready in tiles:
                            products(1 - c % 2, 0, w, True, False, ready)
                return lambda: load_out(BATCH - 1, 1)

            pe.wait_ge(llo_done, 3 * 4)
            with pe.Fori(0, 2) as i:
                for cc in range(2):
                    ffn_chunk(2 * i + cc, 2 * i + cc, cc, False)
            pe.wait_ge(mem_lo, 4)
            last_load_out = memory_phase()
            for c in range(BATCH):
                ffn_chunk(2 * BATCH + c, BATCH + c, c % 2, c == BATCH - 1, last_load_out if c == 0 else None)

        @block.scalar
        def _(act):
            def hi(dst, src, scale=1.0):
                return nc.scalar.activation(dst, src, ACT.Copy, scale=scale)

            def ln_evacuate(L, dt, bank):
                act.wait_ge(lnT_ready, 2 * L + dt + 1)
                act.wait_ge(x_lo, 2 * L - 1 + dt)
                hi(xf[:, dt, :], bank).then_inc(x_f, 1)

            def ln_hi(L, dt, par):
                act.wait_ge(x_f, 2 * L + dt + 1)
                hi(xTh[:, par, dt, :], xf[:, dt, :]).then_inc(x_hi, 1)

            def qk_evacuate(b, n):
                act.wait_ge(qk_ready, 4 * b + n + 1)
                act.wait_ge(qk_lo, 4 * b + n - 1)
                nc.scalar.activation(qf[:, n % 2, :], MB, ACT.Identity, bias=bqk[:, n:n + 1]).then_inc(qk_f, 1)

            def qk_split(b, n):
                act.wait_ge(qk_f, 4 * b + n + 1)
                act.wait_ge(scr_out[n % 2], 2 * DMA * (2 * b + n // 2))
                hi(qh[:, n % 2, :], qf[:, n % 2, :]).then_inc(qk_hi, 1)

            def v_evacuate(b, half, bank=MB, fresh=False):
                act.wait_ge(v_ready, 2 * b + half + 1)
                if not fresh:
                    act.wait_ge(vp_ready, 4 * b)
                hi(vst[:, 2 * half:2 * half + 2, :].rearrange("p t n -> p (t n)"), bank).then_inc(v_copied, 1)

            act.wait_ge(wqk_in, 2 * DMA)
            for i in range(2):
                hi(WAh[:, i, :, :].rearrange("p k n -> p (k n)"), qf[:, i, :]).then_inc(whi_done, 1)
            act.wait_ge(wv_in, DMA)
            hi(WAh[:, 2, :, :].rearrange("p k n -> p (k n)"), xf[:, 0, :]).then_inc(whi_done, 1)
            act.wait_ge(wlo_done, 3)
            for dt in range(KD):
                act.wait_ge(lnT_ready, dt + 1)
                hi(xTh[:, 0, dt, :], PS[:, dt, :]).then_inc(x_hi, 1)
            act.wait_ge(bias_in, DMA)
            for n in range(4):
                if n == 2:
                    act.wait_ge(had_ready, 1)
                    for j in range(FT // 2):
                        last = hi(PR[:, j, :], PS[:, (0, 1, 6, 7)[j], :], 1.0 / HID ** 0.5)
                    last.then_inc(had_copied, 1)
                act.wait_ge(qk_ready, n + 1)
                if n > 1:
                    act.wait_ge(scr_out[n % 2], 2 * DMA)
                nc.scalar.activation(qh[:, n % 2, :], PS[:, 2 + n, :], ACT.Identity, bias=bqk[:, n:n + 1]).then_inc(qk_hi, 1)
            act.wait_ge(wo_in, DMA)
            hi(WOh[:, :, :].rearrange("p g n -> p (g n)"), vst[:, :, :].rearrange("p t n -> p (t n)")).then_inc(whi_done, 1)
            act.wait_ge(wol_done, 1)
            for half in range(2):
                v_evacuate(0, half, PS[:, half, :], True)
            act.wait_ge(fly_done, 3)

            def slot(b, k, first, last):
                g, i = k // 16, k % 16
                act.wait_ge(st_ready, SLOTS * b + k + 1)
                if k % 4 == 0 and not (first and k < 8):
                    act.wait_ge(av_done, 16 * b + k // 4 - 1)
                if k == 4 and first:
                    act.wait_ge(scr_w[W_DOWN], DMA)
                nc.scalar.activation(PR[:, k % 8, :], PS[:, k % 3, :], ACT.Exp, scale=HD ** -0.5).then_inc(exp_done, 1)
                if i == OUT_SLOT + 4 and not (first and g == 0):
                    act.wait_ge(aof_ready, 4 * b + g)
                    hi(AOh[:, (g - 1) % GROUPS, :], AOf[:, :]).then_inc(aoh_done, 1)
                for dt in range(KD):
                    if k == LN_PE[dt] + LN_LATER * last:
                        ln_evacuate(b + 1, dt, MB)
                    if k == LN_PE[dt] + LN_LATER * last + 1:
                        ln_hi(b + 1, dt, 0)
                if not last:
                    for n, k0 in enumerate(QK_PE):
                        if k == k0 + 2:
                            qk_evacuate(b + 1, n)
                        if k == k0 + 3:
                            qk_split(b + 1, n)
                    if k - 2 in V_PE:
                        v_evacuate(b + 1, V_PE.index(k - 2))

            def tail(b):
                act.wait_ge(aof_ready, 4 * b)
                hi(AOh[:, GROUPS - 1, :], AOf[:, :]).then_inc(aoh_done, 1)

            windows(act, slot, tail)

            def ffn_chunk(n, f0, par, last):
                for f in range(FT):
                    act.wait_ge(g_ready, FT * f0 + f + 1)
                    nc.scalar.activation(PR[:, f % 2, :], PS[:, f % 2, :], ACT.Silu).then_inc(sg_done, 1)
                    act.wait_ge(hf_done, FT * f0 + f + 3)
                    hi(AOh[:, f % 4, :], PR[:, 2 + f % 2, :]).then_inc(hh_done, 1)
                    if f == 5 and not last:
                        for dt in range(KD):
                            ln_evacuate(n + BATCH + 1, dt, PS[:, 6 + dt, :])
                            ln_hi(n + BATCH + 1, dt, 1 - par)

            def mem_chunk(n, par):
                c0 = n - BATCH
                def sigmoid(dst, bank, bias, ready, m, done):
                    act.wait_ge(ready, KD * c0 + m + 1)
                    nc.scalar.activation(dst, bank, ACT.Sigmoid, bias=bias).then_inc(done, 1)

                def gate(m):
                    sigmoid(PR[:, m, :], PS[:, 3 * m + 1, :], bgq[:, m:m + 1], bg_ready, m, bsg_done)

                def query(m):
                    sigmoid(PR[:, 2 + m, :], PS[:, 3 * m + 2, :], bgq[:, 2 + m:3 + m], bq_ready, m, bsq_done)

                def load_hi(m):
                    act.wait_ge(load_done, KD * c0 + m + 1)
                    hi(AOh[:, m, :], PR[:, 4 + m, :]).then_inc(lh_done, 1)

                gate(0)
                query(0)
                gate(1)
                load_hi(0)
                for dt in range(KD):
                    ln_evacuate(n + BATCH + 1, dt, PS[:, 6 + dt, :])
                for dt in range(KD):
                    ln_hi(n + BATCH + 1, dt, 1 - par)
                query(1)
                load_hi(1)

            with act.Fori(0, 2) as i:
                for cc in range(2):
                    ffn_chunk(2 * i + cc, 2 * i + cc, cc, False)
            with act.Fori(0, 2) as i:
                for cc in range(2):
                    mem_chunk(BATCH + 2 * i + cc, cc)
            for c in range(BATCH):
                ffn_chunk(2 * BATCH + c, BATCH + c, c % 2, c == BATCH - 1)

        @block.vector
        def _(dve):
            def pause():
                nc.vector.memset(spare[:, :], 0.0)

            def tile_statistics(x_tile, column):
                return nc.vector.bn_stats(bst[:, column, :], X[:, x_tile, :])

            def moments(n0, count, n):
                dve.wait_ge(bst_done, n)
                pause()
                for t in range(count):
                    last = nc.vector.bn_aggr(mom[:, n0 + t, :], bst[:, n0 + t, :])
                last.then_inc(mom_done, 1)

            def statistics(X0, n0, count, n):
                for t in range(count):
                    last = tile_statistics(X0 + t, n0 + t)
                last.then_inc(bst_done, 1)
                moments(n0, count, n)

            def normalise_tile(x_tile, column, t):
                return nc.vector.tensor_scalar(XNs[:, t, :], X[:, x_tile, :], mom[:, bass.ds(column, 1), 0],
                                               rstd[:, bass.ds(column, 1)], ALU.subtract, ALU.mult)

            def normalise(X0, n0, L, fresh=False):
                if not fresh:
                    dve.wait_ge(lnT_ready, 2 * L)
                for t in range(TT):
                    last = normalise_tile(X0 + t, n0 + t, t)
                last.then_inc(xns_ready, 1)

            def lo(dst, src, h):
                return nc.vector.tensor_tensor(dst, src, h.bitcast(F32), ALU.subtract)

            nc.vector.memset(AOf[:, :], 1.0).then_inc(one_done, 1)
            nc.vector.memset(OTn[:, :, :], 0.0).then_inc(zero_done, 1)
            nc.vector.memset(decay[:, :], DECAY)
            dve.wait_ge(x_in[0], DMA)
            statistics(0, 0, TT, 1)
            for i in range(3):
                if i == 2:
                    dve.wait_ge(rstd_done, 1)
                    normalise(0, 0, 0, True)
                dve.wait_ge(whi_done, i + 1)
                raw = xf[:, 0, :] if i == 2 else qf[:, i, :]
                lo(WAl[:, i, :, :].rearrange("p k n -> p (k n)"), raw, WAh[:, i, :, :].rearrange("p k n -> p (k n)"))\
                    .then_inc(wlo_done, 1)
            dve.wait_ge(wlo_done, 3)
            for dt in range(KD):
                dve.wait_ge(x_hi, dt + 1)
                nc.vector.tensor_copy(xf[:, dt, :], PS[:, dt, :]).then_inc(x_f, 1)
            for dt in range(KD):
                dve.wait_ge(x_f, dt + 1)
                lo(xTl[:, 0, dt, :], xf[:, dt, :], xTh[:, 0, dt, :]).then_inc(x_lo, 1)
            for n in range(4):
                if n == 2:
                    for b in range(1, BATCH):
                        dve.wait_ge(x_in[b], DMA)
                    statistics(TT, TT, (BATCH - 1) * TT, 2)
                if n == 0:
                    dve.wait_ge(bias_in, DMA)
                else:
                    dve.wait_ge(qk_lo, n)
                dve.wait_ge(qk_hi, n + 1)
                nc.vector.tensor_scalar(qf[:, n % 2, :], PS[:, 2 + n, :], bqk[:, n:n + 1], None, ALU.add).then_inc(qk_f, 1)
                dve.wait_ge(qk_f, n + 1)
                lo(ql[:, n % 2, :], qf[:, n % 2, :], qh[:, n % 2, :]).then_inc(qk_lo, 1)

            def row_max(b, kk):
                dve.wait_ge(s1_ready, SLOTS * b + kk + 1)
                nc.vector.tensor_reduce(mxr[:, kk // 16 % 2, kk % 16:kk % 16 + 1], PS[:, 3 + kk % 3, :], AX.X, ALU.max)\
                    .then_inc(max_done, 1)

            def split_max(b, g):
                s, m = 4 * b + g, mxr[:, g % 2, :]
                dve.wait_ge(max_done, 16 * s + 16)
                nc.vector.tensor_scalar(ms[:, 0, :].bitcast(F32R), m, -1.0, None, ALU.mult).then_inc(mh_done, 1)
                dve.wait_ge(mh_done, s + 1)
                nc.vector.scalar_tensor_tensor(ms[:, 1, :], m, -1.0, ms[:, 0, :], ALU.mult, ALU.subtract)\
                    .then_inc(ml_done, 1)

            def transpose_max(s, first=False):
                dve.wait_ge(ml_done, s + 1)
                if not first:
                    dve.wait_ge(mscr_out, DMA * s)
                nc.vector.transpose(mT[:, :], ms[:, :, :].rearrange("p a k -> p (a k)")).then_inc(mt_ready, 1)

            def maxima(b, kk, fresh=False):
                row_max(b, kk)
                if kk % 16 == 15:
                    split_max(b, kk // 16)
                    transpose_max(4 * b + kk // 16, fresh)

            for kk in range(AHEAD):
                maxima(0, kk, True)

            def outputs(s, step):
                if step == 0:
                    dve.wait_ge(av_done, 4 * s)
                    nc.vector.transpose(OT[:, :, :].rearrange("p a c -> p (a c)"), OB).then_inc(ot_done, 1)
                elif step == 1:
                    dve.wait_ge(ot_done, s)
                    nc.vector.reciprocal(rec[:, :], OT[:, :, HD]).then_inc(rec_done, 1)
                elif step == 2:
                    dve.wait_ge(otn_done, s)
                    dve.wait_ge(aol_done, s)
                    nc.vector.transpose(AOf[:, :], OTn[:, :, :].rearrange("p a c -> p (a c)")).then_inc(aof_ready, 1)

            def w_split(w, i):
                if i == 0:
                    dve.wait_ge(w_in[w], DMA)
                h, raw = quarter(w, i)
                nc.vector.tensor_copy(h, raw.bitcast(F32)).then_inc(lhi_done, 1)
                if w != W_UP:
                    dve.wait_ge(lhi_done, 4 * w + i + 1)
                    lo(raw, raw.bitcast(F32), h).then_inc(llo_done, 1)

            def add_attention(b, half, bank=MB):
                dve.wait_ge(wo_ready, 2 * b + half + 1)
                dve.wait_ge(bo_added, b + 1)
                v = X[:, bass.ds(TT * b + 2 * half, 2), :].rearrange("p t n -> p (t n)")
                nc.vector.tensor_tensor(v, v, bank, ALU.add).then_inc(x_done, 1)

            def slot(b, k, first, last):
                g, i = k // 16, k % 16
                kk = k + AHEAD
                if k in OUT_ADD and not first:
                    add_attention(b - 1, OUT_ADD.index(k))
                if first and k == TURN - 1:
                    dve.wait_ge(fill_in[GROUPS - 1], 2 * DMA)
                    dve.wait_ge(rstd_done, 2)
                if OUT_SLOT <= i < OUT_SLOT + 3 and not (first and g == 0):
                    outputs(4 * b + g, i - OUT_SLOT)
                if kk < SLOTS:
                    maxima(b, kk)
                elif not last:
                    maxima(b + 1, kk - SLOTS)
                if k == TURN and not last:
                    normalise(TT * (b + 1), TT * (b + 1), b + 1)
                if last:
                    if k in STAT_AT:
                        t = STAT_AT.index(k)
                        if t == 0:
                            dve.wait_ge(x_done, 2 * b)
                        done = tile_statistics(t, t)
                        if t == TT - 1:
                            done.then_inc(bst_done, 1)
                    if k == STAT_AT[-1] + 1:
                        moments(0, TT, 3)
                    if k in NORM_AT:
                        t = NORM_AT.index(k)
                        if t == 0:
                            dve.wait_ge(rstd_done, 3)
                            dve.wait_ge(lnT_ready, 2 * BATCH)
                        done = normalise_tile(t, t, t)
                        if t == TT - 1:
                            done.then_inc(xns_ready, 1)
                if last and k in SPLIT_AT:
                    w_split(*divmod(SPLIT_AT.index(k), 4))

            def tail(b):
                for step in range(3):
                    outputs(4 * b, step)
                for half in range(2):
                    add_attention(b - 1, half, PS[:, (7, 5)[half], :])

            windows(dve, slot, tail)

            def prepare(n, X0):
                statistics(X0, 0, TT, n + 4)

            def ffn_chunk(n, f0, c4, X0, last, split_mem=False, prepared=False):
                for f in range(FT):
                    dve.wait_ge(u_ready, FT * f0 + f + 1)
                    dve.wait_ge(sg_done, FT * f0 + f + 1)
                    nc.vector.tensor_tensor(PR[:, 2 + f % 2, :], PR[:, f % 2, :], PS[:, 2 + f % 2, :], ALU.mult)\
                        .then_inc(hf_done, 1)
                    dve.wait_ge(hh_done, FT * f0 + f + 1)
                    lo(AOl[:, f % 4, :], PR[:, 2 + f % 2, :], AOh[:, f % 4, :]).then_inc(hl_done, 1)
                    if f == 1 and not last and not prepared:
                        dve.wait_ge(x_done, 2 * (n + BATCH))
                        pause()
                        prepare(n, X0)
                    if f == 3 and not last:
                        dve.wait_ge(rstd_done, n + 4)
                        normalise(X0, 0, n + BATCH + 1)
                    if split_mem and f == 5:
                        dve.wait_ge(w_in[W_MEM], DMA)
                        h, raw = (v[:, bass.ds(n * SEQ, SEQ)] for v in parts(W_MEM))
                        nc.vector.tensor_copy(h, raw.bitcast(F32)).then_inc(mem_hi, 1)
                    if split_mem and f == 6:
                        dve.wait_ge(mem_hi, n + 1)
                        lo(raw, raw.bitcast(F32), h).then_inc(mem_lo, 1)
                add_output(n, c4, 4)

            def add_output(n, c4, bank):
                for half in range(2):
                    dve.wait_ge(y_ready, 2 * n + half + 1)
                    v = X[:, bass.ds(c4 + 2 * half, 2), :].rearrange("p t n -> p (t n)")
                    nc.vector.tensor_tensor(v, v, PS[:, bank + half, :], ALU.add).then_inc(x_done, 1)

            def mem_chunk(n, c4, X0, X1):
                c0 = n - BATCH
                for m in range(KD):
                    dve.wait_ge(bsg_done, KD * c0 + m + 1)
                    dve.wait_ge(bv_ready, KD * c0 + m + 1)
                    store, mem = PR[:, 4 + m, :], PR[:, 6 + m, :]
                    nc.vector.scalar_tensor_tensor(store, PS[:, 3 * m, :], MSCALE, PR[:, m, :], ALU.mult, ALU.mult)\
                        .then_inc(bst2_done, 1)
                    dve.wait_ge(bst2_done, KD * c0 + m + 1)
                    nc.vector.tensor_tensor_scan(mem, decay[:, 0:1].broadcast_to([P, SEQ]), store, 0.0, ALU.mult, ALU.add)\
                        .then_inc(scan_done, 1)
                    if m == 0:
                        dve.wait_ge(rstd_done, n + 4)
                        normalise(X0, 0, n + BATCH + 1)
                    dve.wait_ge(scan_done, KD * c0 + m + 1)
                    dve.wait_ge(bsq_done, KD * c0 + m + 1)
                    nc.vector.scalar_tensor_tensor(store, mem, MSCALE, PR[:, 2 + m, :], ALU.mult, ALU.mult)\
                        .then_inc(load_done, 1)
                    dve.wait_ge(lh_done, KD * c0 + m + 1)
                    lo(AOl[:, m, :], store, AOh[:, m, :]).then_inc(ll_done, 1)
                    if m:
                        dve.wait_ge(x_done, 2 * (n + BATCH))
                        pause()
                        prepare(n + 1, X1)
                add_output(n, c4, 6)

            def following(i, cc):
                return TT * (2 * i + 1) if cc == 0 else 2 * TT * (1 - i)

            with dve.Fori(0, 2) as i:
                for cc in range(2):
                    ffn_chunk(2 * i + cc, 2 * i + cc, TT * (2 * i + cc), following(i, cc), False, True)
            dve.wait_ge(x_done, 4 * BATCH)
            prepare(BATCH, TT)
            with dve.Fori(0, 2) as i:
                for cc in range(2):
                    mem_chunk(BATCH + 2 * i + cc, TT * (2 * i + cc), following(i, cc),
                              2 * TT * (1 - i) if cc == 0 else TT * (3 - 2 * i))
            for c in range(BATCH):
                ffn_chunk(2 * BATCH + c, BATCH + c, TT * c, TT * ((c + 1) % BATCH), c == BATCH - 1, False, c == 0)

        @block.gpsimd
        def _(pool):
            def reciprocal_deviation(n0, count, n):
                pool.wait_ge(mom_done, n)
                nc.gpsimd.tensor_tensor(veps[:, n0:n0 + count], mom[:, n0:n0 + count, 1], eps[:, n0:n0 + count], ALU.add)\
                    .then_inc(veps_done, 1)
                pool.wait_ge(veps_done, n)
                nc.gpsimd.tensor_tensor(rstd[:, n0:n0 + count], veps[:, n0:n0 + count], mhalf[:, n0:n0 + count], ALU.pow)\
                    .then_inc(rstd_done, 1)

            def lo(dst, src, h):
                return nc.gpsimd.tensor_tensor(dst, src, h.bitcast(F32), ALU.subtract)

            def x_lo_part(L, dt, par):
                pool.wait_ge(x_hi, 2 * L + dt + 1)
                lo(xTl[:, par, dt, :], xf[:, dt, :], xTh[:, par, dt, :]).then_inc(x_lo, 1)

            def qk_lo_part(b, n):
                pool.wait_ge(qk_hi, 4 * b + n + 1)
                lo(ql[:, n % 2, :], qf[:, n % 2, :], qh[:, n % 2, :]).then_inc(qk_lo, 1)

            def place_values(b, g, fresh=False):
                pool.wait_ge(v_copied, 2 * b + 2)
                if not fresh:
                    pool.wait_ge(av_done, 16 * b + 4 * g - 12)
                cs = slice(g * GH * HD, (g + 1) * GH * HD)
                nc.gpsimd.tensor_tensor(Vp[:, :, GH * g:GH * (g + 1), 0:HD],
                                        vst[:, :, cs].rearrange("p t (h c) -> p t h c", c=HD),
                                        bvt[:, cs].rearrange("p (h c) -> p h c", c=HD).unsqueeze(1)
                                        .broadcast_to([P, TT, GH, HD]), ALU.add).then_inc(vp_ready, 1)

            def divide(s):
                pool.wait_ge(rec_done, s)
                nc.gpsimd.tensor_tensor(OTn[:, :, 0:HD], OT[:, :, 0:HD],
                                        rec[:, :].unsqueeze(2).broadcast_to([P, SEQ // 32, HD]), ALU.mult)\
                    .then_inc(otn_done, 1)

            def output_lo(s, g):
                pool.wait_ge(aoh_done, s)
                lo(AOl[:, g, :], AOf[:, :], AOh[:, g, :]).then_inc(aol_done, 1)

            def add_bo(b):
                v = X[:, bass.ds(TT * b, TT), :]
                nc.gpsimd.tensor_tensor(v, v, bot[:, :].unsqueeze(1).broadcast_to([P, TT, D]), ALU.add).then_inc(bo_added, 1)

            nc.gpsimd.memset(mhalf[:, :], -0.5)
            nc.gpsimd.memset(eps[:, :], EPS).then_inc(pool_init, 1)
            nc.gpsimd.memset(Vp[:, :, :, HD:HD + 1], 1.0).then_inc(pool_init, 1)
            nc.gpsimd.memset(Vp[:, :, :, HD + 1:], 0.0).then_inc(hf_done, 2)
            pool.wait_ge(pool_init, 2)
            reciprocal_deviation(0, TT, 1)
            pool.wait_ge(had_copied, 1)
            for st in range(3):
                r = 1 << st
                src, dst = (PR[:, 4 * h:4 * h + 4, :].rearrange("p a n -> p (a n)")
                            .rearrange("p (m u r) -> p m u r", u=2, r=r * D) for h in (st % 2, 1 - st % 2))
                if st:
                    pool.wait_ge(fly_done, st)
                nc.gpsimd.tensor_tensor(dst[:, :, 0, :], src[:, :, 0, :], src[:, :, 1, :], ALU.add)
                nc.gpsimd.tensor_tensor(dst[:, :, 1, :], src[:, :, 0, :], src[:, :, 1, :], ALU.subtract).then_inc(fly_done, 1)
            pool.wait_ge(whi_done, 4)
            lo(WOl[:, :, :].rearrange("p g n -> p (g n)"), vst[:, :, :].rearrange("p t n -> p (t n)"),
               WOh[:, :, :].rearrange("p g n -> p (g n)")).then_inc(wol_done, 1)
            pool.wait_ge(const_in, 3 * DMA)
            for g in range(GROUPS):
                place_values(0, g, True)
            reciprocal_deviation(TT, (BATCH - 1) * TT, 2)
            pool.wait_ge(xns_ready, 1)
            add_bo(0)

            def slot(b, k, first, last):
                g, i = k // 16, k % 16
                if first and k == TURN - 1:
                    pool.wait_ge(fill_in[GROUPS - 1], 2 * DMA)
                if i == OUT_SLOT + 1 and not (first and g == 0):
                    divide(4 * b + g)
                if k == OUT_SLOT + 4 and not first:
                    output_lo(4 * b, GROUPS - 1)
                if k == 9 and not first:
                    place_values(b, GROUPS - 1)
                if k == 50 and not last:
                    pool.wait_ge(xns_ready, b + 2)
                    add_bo(b + 1)
                if k == STAT_AT[-1] + 2 and last:
                    reciprocal_deviation(0, TT, 3)
                for dt in range(KD):
                    if k == LN_PE[dt] + LN_LATER * last + 1:
                        x_lo_part(b + 1, dt, 0)
                if k > 16 and i == OUT_SLOT + 4:
                    output_lo(4 * b + k // 16, k // 16 - 1)
                if not last:
                    if k - 3 in QK_PE:
                        qk_lo_part(b + 1, QK_PE.index(k - 3))
                    if k in V_PLACE:
                        place_values(b + 1, V_PLACE.index(k))

                if last and k in SPLIT_AT[:4]:
                    n = SPLIT_AT.index(k)
                    pool.wait_ge(lhi_done, n + 1)
                    h, raw = quarter(W_UP, n)
                    lo(raw, raw.bitcast(F32), h).then_inc(llo_done, 1)

            nc.gpsimd.memset(credit[:, :], 0.0).then_inc(aol_done, 1)
            def tail(b):
                divide(4 * b)
                output_lo(4 * b, GROUPS - 1)

            windows(pool, slot, tail)

            def prepare(n, par):
                reciprocal_deviation(0, TT, n + 4)
                for dt in range(KD):
                    x_lo_part(n + BATCH + 1, dt, 1 - par)

            for n0 in (0, BATCH):
                with pool.Fori(0, 2) as i:
                    for cc in range(2):
                        prepare(n0 + 2 * i + cc, cc)
            for c in range(BATCH - 1):
                prepare(2 * BATCH + c, c % 2)


def kernel(**inputs):
    import numpy as np
    import concourse.bacc as bacc
    from concourse import mybir as mb
    from concourse.bass_utils import run_bass_kernel_spmd as run

    a = {k.split("_", 1)[1]: np.asarray(v) for k, v in inputs.items()}
    order = np.arange(D).reshape(2, HEADS // 2, HD).transpose(0, 2, 1).reshape(-1)
    wo = np.zeros((GROUPS, GH, 32, D), np.float32)
    wo[:, :, :HD, :] = a["attn_a_Wo"].T.reshape(GROUPS, GH, HD, D)
    bqk = np.stack([a["attn_a_bq"][order].reshape(KD, P), a["attn_a_bk"][order].reshape(KD, P)], 1).reshape(2 * KD, P).T
    bgq = np.concatenate([a["attn_b_bg"].reshape(KD, P), a["attn_b_bq"].reshape(KD, P)]).T
    had = np.ones((1, 1), np.float32)
    while had.shape[0] < P:
        had = np.block([[had, had], [had, -had]])
    arrays = {
        "x": a["attn_a_x"], "wq": a["attn_a_Wq"].T[:, order], "wk": a["attn_a_Wk"].T[:, order],
        "wv": a["attn_a_Wv"].T, "wo": wo.reshape(GROUPS, P, D), "bqk_d": bqk, "bgq_d": bgq, "bv": a["attn_a_bv"], "bo": a["attn_a_bo"],
        "mv_": a["attn_b_Wv"], "mg": a["attn_b_Wg"], "mq": a["attn_b_Wq"], "mo": a["attn_b_Wo"], "w1": a["ffn_W1"].T, "w2": a["ffn_W2"].T,
        "w3": a["ffn_W3"].T, "ident_d": np.eye(P, dtype=np.float32), "had_d": had.astype(np.float32),
    }
    arrays = {k: np.ascontiguousarray(v) for k, v in arrays.items()}
    nc = bacc.Bacc("TRN2", target_bir_lowering=False, num_devices=1)
    args = {k: nc.dram_tensor(f"in_{k}", v.shape, mb.dt.from_np(v.dtype), kind="ExternalInput").ap()
            for k, v in arrays.items()}
    args["out"] = nc.dram_tensor("out_0", [BATCH, SEQ, D], F32, kind="ExternalOutput").ap()
    build(nc, **args)
    got = run(nc, [{f"in_{k}": v for k, v in arrays.items()}], core_ids=[0])
    return got.results[0]["out_0"]
```
